# Optimizing a Trainium2 kernel written in Bass

```python
import numpy as np
import jax
import jax.numpy as jnp

def _softmax(x, axis=-1):
    return jax.nn.softmax(x, axis=axis)

def _gelu(x):
    return jax.nn.gelu(x, approximate=True)

def _silu(x):
    return jax.nn.silu(x)

def _sigmoid(x):
    return jax.nn.sigmoid(x)

def _layernorm(x, axis=-1, eps=1e-05):
    m = jnp.mean(x, axis=axis, keepdims=True)
    v = jnp.var(x, axis=axis, keepdims=True)
    return (x - m) / jnp.sqrt(v + eps)

def _scatter_add(tgt, idx, src, axis=0):
    return tgt.at[idx].add(src)

def _segment_sum(src, seg, n):
    return jax.ops.segment_sum(src, seg, n)
kernel_name = 'mk_adaln_d1_jaxref_r8_941446'

def setup_inputs(seed: int=0):
    np.random.seed(seed)
    _w = jnp.asarray

    def _L0_attn_setup():
        import jax, jax.numpy as jnp
        import numpy as np
        B, S, D, DV = (1, 512, 128, 128)
        key = jax.random.key(seed)
        kq, kk, kv, ks, kp = jax.random.split(key, 5)
        return {'q': jax.random.normal(kq, (B, S, D), dtype=jnp.float32), 'k': jax.random.normal(kk, (B, S, D), dtype=jnp.float32), 'v': jax.random.normal(kv, (B, S, DV), dtype=jnp.float32), 'scale_factor': jax.random.normal(ks, (1,), dtype=jnp.float32), 'dropout_p': jax.random.uniform(kp, (1,), dtype=jnp.float32)}
    _L0_attn_in = _L0_attn_setup()

    def _L0_ffn_setup():
        import jax, jax.numpy as jnp
        import numpy as np
        from jax import lax
        D = 128
        H = 512
        E = 8
        TOPK = 2
        key = jax.random.key(seed)
        ks = jax.random.split(key, 7)
        s = 0.02
        return {'x': jax.random.normal(ks[0], (2, 256, D), dtype=jnp.float32), 'W1': jax.random.normal(ks[1], (E, D, H), dtype=jnp.float32) * s, 'b1': jnp.zeros((E, H), dtype=jnp.float32), 'W2': jax.random.normal(ks[2], (E, H, D), dtype=jnp.float32) * s, 'b2': jnp.zeros((E, D), dtype=jnp.float32), 'Wr': jax.random.normal(ks[3], (D, E), dtype=jnp.float32) * s, 'br': jnp.zeros((E,), dtype=jnp.float32)}
    _L0_ffn_in = _L0_ffn_setup()
    _L0_c = _w((lambda *s: np.random.randn(*s).astype(np.float32) * 0.05)(4, 128))
    _L0_wmod = _w((lambda *s: np.random.randn(*s).astype(np.float32) * 0.05)(128, 6 * 128) * 128 ** (-0.5))
    _d = {'L0_attn_q': _L0_attn_in['q'], 'L0_attn_k': _L0_attn_in['k'], 'L0_attn_v': _L0_attn_in['v'], 'L0_attn_scale_factor': _L0_attn_in['scale_factor'], 'L0_attn_dropout_p': _L0_attn_in['dropout_p'], 'L0_ffn_W1': _L0_ffn_in['W1'], 'L0_ffn_b1': _L0_ffn_in['b1'], 'L0_ffn_W2': _L0_ffn_in['W2'], 'L0_ffn_b2': _L0_ffn_in['b2'], 'L0_ffn_Wr': _L0_ffn_in['Wr'], 'L0_ffn_br': _L0_ffn_in['br'], 'L0_c': _L0_c, 'L0_wmod': _L0_wmod}
    _x0 = _d['L0_attn_q']
    _d['L0_attn_q'] = jax.random.normal(jax.random.fold_in(jax.random.key(seed), 1), (4, 1024, 128), dtype=_x0.dtype)
    del _x0
    return _d

def reference(L0_attn_q, L0_attn_k, L0_attn_v, L0_attn_scale_factor, L0_attn_dropout_p, L0_ffn_W1, L0_ffn_b1, L0_ffn_W2, L0_ffn_b2, L0_ffn_Wr, L0_ffn_br, L0_c, L0_wmod):

    def _L0_attn_ref(q, k, v, scale_factor, dropout_p):
        import jax, jax.numpy as jnp
        import numpy as np
        B, S, D, DV = (1, 512, 128, 128)
        b, s, d = q.shape
        step = s // 4
        scale = q[:, ::step].reshape(b, -1)
        qk = jnp.einsum('bsd,btd->bst', q, k)
        scaled_qk = qk * scale[:, None, :]
        softmax_qk = jax.nn.softmax(scaled_qk, axis=-1)
        return jnp.einsum('bst,btv->bsv', softmax_qk, v)

    def _L0_ffn_ref(x, W1, b1, W2, b2, Wr, br):
        import jax, jax.numpy as jnp
        import numpy as np
        from jax import lax
        D = 128
        H = 512
        E = 8
        TOPK = 2
        B, S, _ = x.shape
        xf = x.reshape(-1, D)
        logits = xf @ Wr + br
        topv, _ = lax.top_k(logits, TOPK)
        thresh = topv[:, TOPK - 1:TOPK]
        masked = jnp.where(logits >= thresh, logits, -jnp.inf)
        weights = jax.nn.softmax(masked, axis=-1)
        h = jax.nn.gelu(jnp.einsum('td,edh->eth', xf, W1) + b1[:, None, :], approximate=False)
        expert_out = jnp.einsum('eth,ehd->etd', h, W2) + b2[:, None, :]
        out = jnp.einsum('etd,te->td', expert_out, weights)
        return out.reshape(B, S, D)
    x = L0_attn_q
    mod = (_silu(L0_c) @ L0_wmod).reshape(L0_c.shape[0], 6, 1, -1)
    sa, ca, ga, sb, cb, gb = (mod[:, 0], mod[:, 1], mod[:, 2], mod[:, 3], mod[:, 4], mod[:, 5])
    ga = (2 * (ga >= 0) - 1) * jnp.maximum(jnp.abs(ga), 0.25)
    gb = (2 * (gb >= 0) - 1) * jnp.maximum(jnp.abs(gb), 0.25)
    h = _layernorm(x, axis=-1) * (1 + ca) + sa
    x = x + ga * _L0_attn_ref(h, L0_attn_k, L0_attn_v, L0_attn_scale_factor, L0_attn_dropout_p)
    h = _layernorm(x, axis=-1) * (1 + cb) + sb
    x = x + gb * _L0_ffn_ref(h, L0_ffn_W1, L0_ffn_b1, L0_ffn_W2, L0_ffn_b2, L0_ffn_Wr, L0_ffn_br)
    return x

_drawn_inputs = setup_inputs


def setup_inputs(seed=0):
    import zlib

    import numpy as np

    out = dict(_drawn_inputs(seed))
    spreads = {'L0_ffn_b1': (0.0, 0.8), 'L0_ffn_b2': (0.0, 0.5), 'L0_ffn_br': (0.0, 0.47)}
    factors = {'L0_ffn_W1': 6.13, 'L0_ffn_W2': 5.546, 'L0_ffn_Wr': 3.745}
    for name, (base, spread) in spreads.items():
        noise = np.random.default_rng([zlib.crc32(name.encode()), seed]).standard_normal(out[name].shape)
        drawn = base * np.exp(spread * noise) if base else spread * noise
        out[name] = jnp.asarray(drawn.astype(out[name].dtype))
    for name, factor in factors.items():
        out[name] = (out[name] * factor).astype(out[name].dtype)
    return out
```

```python
from contextlib import ExitStack

import concourse.bass as bass
from concourse import mybir

ALU = mybir.AluOpType
ACT = mybir.ActivationFunctionType
F32 = mybir.dt.float32
F32R = mybir.dt.float32r
AX_X = mybir.AxisListType.X

P = 128
TG = 4
GT = TG * P
SPLIT = 2


def adaln_block(nc, q, k, v, W1, b1, W2, b2, Wr, br, c, wmod, out):
    B, S, D = q.shape
    T = k.shape[1]
    E, _, H = W1.shape
    MODS = wmod.shape[1] // D
    KC = T // P
    HC = H // P
    NT = B * S // P
    NG = NT // TG
    GB = NG // B
    BT = NT // B
    STEP = S // 4
    EPS = 1e-5
    WROWS = 2 * E
    WCH = 4
    EW = E // WCH
    SA, CA, GA, SB, CB, GBM = range(6)
    assert D == P and T == GT and GB == 2 and MODS == 6 and KC == 4 and HC == 4 and E == 8

    with ExitStack() as ctx:
        def sb(name, shape, dt=F32):
            return ctx.enter_context(nc.sbuf_tensor(name, shape, dt))

        def sem(name):
            return ctx.enter_context(nc.semaphore(name))

        x_sb = sb("x_sb", [P, NT, D])
        w1hi = sb("w1hi", [P, E, H], F32R)
        w1lo = sb("w1lo", [P, E, H], F32R)
        w2hi = sb("w2hi", [P, E, HC * D], F32R)
        w2lo = sb("w2lo", [P, E, HC * D], F32R)
        h2hi = sb("h2hi", [P, NT * P], F32R)
        h2lo = sb("h2lo", [P, NT * P], F32R)
        gel = sb("gel", [P, 2, HC, GT])
        sphi = sb("sphi", [P, 2, HC, GT], F32R)
        splo = sb("splo", [P, 2, HC, GT], F32R)
        w2raw = sb("w2raw", [P, 2, EW * HC * D])
        hthi = sb("hthi", [P, GB, GT], F32R)
        htlo = sb("htlo", [P, GB, GT], F32R)
        kthi = sb("kthi", [P, T], F32R)
        ktlo = sb("ktlo", [P, T], F32R)
        vhi = sb("vhi", [P, KC, D], F32R)
        vlo = sb("vlo", [P, KC, D], F32R)
        k_sb = sb("k_sb", [P, KC, D])
        probs = sb("probs", [P, 2, T])
        ks = probs[:, 0, :].rearrange("p (n d) -> p n d", d=D)
        att = sb("att", [P, GT])
        xh = sb("xh", [P, 2, TG, D])
        ht = sb("ht", [P, GB, GT])
        h2 = sb("h2", [P, GT])
        ident = sb("ident", [P, P])
        rows = att[0:E * HC + E + B, 0:P]
        cols = sb("cols", [P, E * HC + E + B])
        wm_sb = gel[:, 1, 0:2, :].rearrange("p a b -> p (a b)")[:, 0:MODS * D]
        sil = sb("sil", [P, 3, B])
        mod = sb("mod", [P, MODS, B])
        gsgn = sb("gsgn", [P, 2, 2, B])
        gb_g = sb("gb_g", [P, NG])
        wr_sb = sb("wr_sb", [P, E])
        br_sb = sb("br_sb", [P, E])
        st = sb("st", [P, 2, TG, 6])
        mv = sb("mv", [P, 2, TG, 2])
        veps = sb("veps", [P, 2, TG])
        rstd = sb("rstd", [P, 2, TG])
        mhalf = sb("mhalf", [P, TG])
        nmax = sb("nmax", [P, GB, TG])
        rsum = sb("rsum", [P, GB, TG])
        rinv = sb("rinv", [P, TG])
        lg = sb("lg", [P, TG, E])
        top = sb("top", [P, TG, 8])
        dlt = sb("dlt", [P, TG, E])
        keep = sb("keep", [P, TG, E])
        ex = sb("ex", [P, TG, E])
        em = sb("em", [P, TG, E])
        esum = sb("esum", [P, TG])
        einv = sb("einv", [P, TG])
        wgt = sb("wgt", [P, TG, E])
        gates = sb("gates", [P, NG, TG * WROWS])
        gcur = sb("gcur", [P, TG * WROWS])
        b1c = cols[:, 0:E * HC]
        b2c = cols[:, E * HC:E * HC + E]
        cc = cols[:, E * HC + E:E * HC + E + B]
        gbc = probs
        msk = w2raw[:, 0, :].rearrange("p (s t) -> p s t", s=2)
        acc = w2raw[:, 1, 0:GT]
        sel32 = ks[0:WROWS, :, :].rearrange("p a b -> p (a b)")
        outT = att
        sel = hthi[0:WROWS, :, :].rearrange("p a (e n) -> p (a e) n", n=P)
        gT = kthi[0:WROWS, :]

        ps = [ctx.enter_context(nc.psum_tensor(f"ps{i}", [P, GT], F32)) for i in range(8)]
        ps_s, ps_pt, ps_av, ps_back, ps_h, ps_log = ps[0:2], ps[2:4], ps[4], ps[5], ps[6], ps[7]
        ps_u, ps_o, ps_gb, ps_x = ps[0:4], ps[4:6], ps[6], ps[7]

        ONE = 1

        rows_in, x_in, wm_in, k_in, v_in, router_in = map(sem, (
            "rows_in", "x_in", "wm_in", "k_in", "v_in", "router_in"))
        x_b = [sem(f"x_in{i}") for i in range(B)]
        w1_in = [sem(f"w1_in{i}") for i in range(WCH)]
        w2_in = [sem(f"w2_in{i}") for i in range(WCH)]
        names = """zeroed ident_ready rows_T cols_ready cexp c1 crec sil_ready mod_ps mod_copied
            mod_ready mod_step gb_ready v_hi v_split w1_hi w1_split w2_hi w2_split
            stat1 aggr1 var1 rstd1 xhat_ready h_ps ht_evac ht_split ks_ready ks_ps kthi_ready
            kt_ready scores_ready nmax_ready exp_done pt_ps pthi_ready pt_split pv_done att_ready
            back_ps x2_done rinv_ready stat2 aggr2 var2 rstd2 xhat2_ready h2_ready h2_hi h2_split
            log_ps lg_ready top_ready dlt_ready keep_ready ex_ready em_ready esum_ready einv_ready
            wgt_ready gate_hi gates_ready xfree""".split()
        s = {n: sem(n) for n in names}

        x_dram = q.rearrange("b s d -> (b s) d").rearrange("(n p) d -> p n d", p=P)
        out_dram = out.rearrange("b s d -> (b s) d").rearrange("(n p) d -> p n d", p=P)
        k_dram = k[0].rearrange("(n p) d -> p n d", p=P)
        v_dram = v[0].rearrange("(n p) d -> p n d", p=P)
        w1_dram = W1.rearrange("e d h -> d e h")
        w2_dram = W2.rearrange("e (c p) d -> p e c d", p=P)
        w1raw = gel[:, :, :, :].rearrange("p a b t -> p (a b t)").rearrange("p (e h) -> p e h", h=H)
        v_raw = probs[:, 1, :].rearrange("p (n d) -> p n d", d=D)

        def wait_all(eng, loaded, value, *counted):
            counted = [(of, n if isinstance(n, int) else eng.to_reg(n)) for of, n in counted]
            eng.wait_ge(loaded, value)
            for of, n in counted:
                eng.wait_ge(of, n)

        with nc.Block() as block:

            @block.sync
            def _(sp):
                sp.dma_start(rows[0:E * HC, :], b1.rearrange("e (c p) -> (e c) p", p=P)).then_inc(rows_in, 16)
                sp.dma_start(rows[E * HC:E * HC + E, :], b2).then_inc(rows_in, 16)
                sp.dma_start(rows[E * HC + E:E * HC + E + B, :], c).then_inc(rows_in, 16)
                for i in range(B):
                    sp.dma_start(x_sb[:, BT * i:BT * (i + 1), :], x_dram[:, BT * i:BT * (i + 1), :]).then_inc(x_b[i], 16)
                sp.wait_ge(s["mod_ps"], 1)
                for i in range(WCH):
                    sp.dma_start(w1raw[:, EW * i:EW * (i + 1), :], w1_dram[:, EW * i:EW * (i + 1), :]).then_inc(w1_in[i], 16)
                for i in range(WCH):
                    if i >= 2:
                        sp.wait_ge(s["w2_split"], i - 1)
                    for j in range(EW):
                        sp.dma_start(w2raw[:, i % 2, j * H:(j + 1) * H].rearrange("p (c d) -> p c d", c=HC),
                                     w2_dram[:, EW * i + j, :, :]).then_inc(w2_in[i], 16)

            @block.gpsimd
            def _(pool):
                pool.sem_inc(s["h2_split"], ONE)
                pool.memset(mhalf[:, :], -0.5).then_inc(s["zeroed"], 1)
                pool.memset(ident[:, :], 0.0).then_inc(s["zeroed"], 1)
                pool.wait_ge(s["zeroed"], 2)
                pool.affine_select(out=ident[:, :], in_=ident[:, :], compare_op=ALU.not_equal, fill=1.0,
                                   base=0, pattern=[[-1, P]], channel_multiplier=1).then_inc(s["ident_ready"], 1)

                def split_w1(i):
                    pool.wait_ge(w1_in[i], 16)
                    e = slice(EW * i, EW * (i + 1))
                    pool.tensor_copy(w1hi[:, e, :], w1raw[:, e, :]).then_inc(s["w1_hi"], 1)
                    pool.wait_ge(s["w1_hi"], i + 1)
                    pool.tensor_tensor(w1lo[:, e, :], w1raw[:, e, :], w1hi[:, e, :].bitcast(F32),
                                       ALU.subtract).then_inc(s["w1_split"], 1)

                def split_w2(i):
                    pool.wait_ge(w2_in[i], 16 * EW)
                    e = slice(EW * i, EW * (i + 1))
                    raw = w2raw[:, i % 2, :].rearrange("p (e n) -> p e n", e=EW)
                    pool.tensor_copy(w2hi[:, e, :], raw).then_inc(s["w2_hi"], 1)
                    pool.wait_ge(s["w2_hi"], i + 1)
                    pool.tensor_tensor(w2lo[:, e, :], raw, w2hi[:, e, :].bitcast(F32),
                                       ALU.subtract).then_inc(s["w2_split"], 1)

                def split_h2(b, g):
                    n = GB * b + g
                    at = slice(n * GT, n * GT + GT) if isinstance(n, int) else bass.ts(n, GT)
                    pool.wait_ge(s["h2_ready"], n + 1)
                    pool.tensor_copy(h2hi[:, at], h2[:, :]).then_inc(s["h2_hi"], 1)
                    pool.wait_ge(s["h2_hi"], n + 1)
                    pool.tensor_tensor(h2lo[:, at], h2[:, :], h2hi[:, at].bitcast(F32),
                                       ALU.subtract).then_inc(s["h2_split"], 1)

                def root(slot, n):
                    pool.wait_ge(s[("var1", "var2")[slot]], n + 1)
                    pool.tensor_tensor(rstd[:, slot, :], veps[:, slot, :], mhalf[:, :], ALU.pow).then_inc(s[("rstd1", "rstd2")[slot]], 1)

                root(0, 0)
                root(0, 1)
                split_w1(0)
                for b in range(B):
                    root(1, GB * b)
                    split_h2(b, 0)
                    if b < B - 1:
                        root(0, GB * (b + 1))
                        root(0, GB * (b + 1) + 1)
                    root(1, GB * b + 1)
                    split_h2(b, 1)
                    if b < B - 1:
                        split_w1(b + 1)
                    split_w2(b)

            @block.tensor
            def _(pe):
                pe.sem_inc(s["back_ps"], ONE)
                pe.sem_inc(s["log_ps"], ONE)
                pe.wait_ge(s["ident_ready"], 1)
                pe.wait_ge(rows_in, 48)
                R = E * HC + E + B
                pe.transpose(ps_back[:, 0:R], rows, ident[0:R, 0:R]).then_inc(s["rows_T"], 1)
                pe.wait_ge(s["sil_ready"], 1)
                pe.wait_ge(wm_in, 16)
                for m in range(MODS):
                    mm = pe.matmul(ps_log[:, m * B:(m + 1) * B], wm_sb[:, m * D:(m + 1) * D], sil[:, 2, :],
                                   start=True, stop=True)
                mm.then_inc(s["mod_ps"], 1)

                def turn_h(slot, ready, count, read=None):
                    pe.wait_ge(s[ready], ONE + count)
                    if read:
                        pe.wait_ge(s[read[0]], read[1])
                    for t in range(TG):
                        mm = pe.transpose(ps_h[:, t * P:(t + 1) * P], xh[:, slot, t, :], ident[:, :])
                    mm.then_inc(s["h_ps"], 1)

                def turn_keys(b):
                    pe.wait_ge(s["ks_ready"], b + 1)
                    pe.wait_ge(s["att_ready"], GB * b)
                    for j in range(KC):
                        mm = pe.transpose(ps_av[:, j * P:(j + 1) * P], ks[:, j, :], ident[:, :])
                    mm.then_inc(s["ks_ps"], 1)

                def scores(b, g, t):
                    if t == 0:
                        pe.wait_ge(s["ht_split"], GB * b + g + 1)
                        pe.wait_ge(s["kt_ready"], b + 1)
                    hi, lo = hthi[:, g, t * P:(t + 1) * P], htlo[:, g, t * P:(t + 1) * P]
                    pe.matmul(ps_s[t % 2][:, :], hi, ktlo[:, :], start=True, stop=False)
                    pe.matmul(ps_s[t % 2][:, :], lo, kthi[:, :], start=False, stop=False)
                    pe.matmul(ps_s[t % 2][:, :], hi, kthi[:, :], start=False, stop=True).then_inc(s["scores_ready"], 1)

                def turn_probs(b, g, t):
                    i = BT * b + TG * g + t
                    pe.wait_ge(s["exp_done"], i + 1)
                    if t >= 2:
                        pe.wait_ge(s["pt_split"], i - 1)
                    for j in range(KC):
                        mm = pe.transpose(ps_pt[t % 2][:, j * P:(j + 1) * P], probs[:, t % 2, j * P:(j + 1) * P],
                                          ident[:, :])
                    mm.then_inc(s["pt_ps"], 1)

                def values(b, g):
                    pe.wait_ge(s["pt_split"], BT * b + TG * (g + 1))
                    if isinstance(b, int) and b == 0 and g == 0:
                        pe.wait_ge(s["v_split"], 1)
                    if g == 1:
                        pe.wait_ge(s["att_ready"], GB * b + g)
                    else:
                        pe.wait_ge(s["v_split"], 1)
                    for n, (w, p) in enumerate(((vlo, sphi), (vhi, splo), (vhi, sphi))):
                        for j in range(KC):
                            mm = pe.matmul(ps_av[:, :], w[:, j, :], p[:, g, j, :],
                                           start=(n == 0 and j == 0), stop=(n == 2 and j == KC - 1))
                    mm.then_inc(s["pv_done"], 1)

                def turn_back(b, g):
                    n = GB * b + g
                    pe.wait_ge(s["att_ready"], n + 1)
                    pe.wait_ge(s["x2_done"], ONE + n)
                    for t in range(TG):
                        mm = pe.transpose(ps_back[:, t * P:(t + 1) * P], att[:, t * P:(t + 1) * P], ident[:, :])
                    mm.then_inc(s["back_ps"], 1)

                def logits(b, g):
                    n = GB * b + g
                    pe.wait_ge(s["h2_ready"], n + 1)
                    pe.wait_ge(s["lg_ready"], ONE + n)
                    if g == 0:
                        pe.wait_ge(router_in, 32)
                    for t in range(TG):
                        mm = pe.matmul(ps_log[:, t * E:(t + 1) * E], h2[:, t * P:(t + 1) * P], wr_sb[:, :],
                                       start=True, stop=True)
                    mm.then_inc(s["log_ps"], 1)

                def group(b, g, between=None):
                    scores(b, g, 0)
                    scores(b, g, 1)
                    turn_probs(b, g, 0)
                    if between:
                        turn_back(b, 0)
                    scores(b, g, 2)
                    turn_probs(b, g, 1)
                    scores(b, g, 3)
                    turn_probs(b, g, 2)
                    turn_probs(b, g, 3)
                    if between:
                        turn_h(1, "xhat2_ready", GB * b + 1, ("ht_evac", GB * (b + 1)))
                    values(b, g)
                    if between:
                        logits(b, 0)

                def batch(b, last):
                    group(b, 0)
                    group(b, 1, True)
                    if not last:
                        turn_h(0, "xhat_ready", GB * (b + 1) + 1, ("h2_ready", GB * b + 1))
                    turn_back(b, 1)
                    if not last:
                        turn_h(0, "xhat_ready", GB * (b + 1) + 2, ("ht_evac", GB * (b + 1) + 1))
                        turn_keys(b + 1)
                    turn_h(1, "xhat2_ready", GB * b + 2,
                           ("h2_ready", GB * b + 1) if last else ("ht_evac", GB * (b + 2)))
                    logits(b, 1)

                turn_h(0, "xhat_ready", 1)
                turn_h(0, "xhat_ready", 2, ("ht_evac", 1))
                turn_keys(0)
                with pe.Fori(0, B - 1) as b:
                    batch(b, False)
                batch(B - 1, True)

            @block.scalar
            def _(act):
                act.dma_start(wm_sb, wmod).then_inc(wm_in, 16)
                act.dma_start(k_sb[:, :, :], k_dram).then_inc(k_in, 16)
                act.dma_start(v_raw, v_dram).then_inc(v_in, 16)
                act.dma_start(wr_sb[:, :], Wr).then_inc(router_in, 16)
                act.dma_start(br_sb[:, :], br.rearrange("(a e) -> a e", a=1).broadcast_to([P, E])).then_inc(router_in, 16)
                act.wait_ge(s["cols_ready"], 1)
                act.activation(sil[:, 0, :], cc, ACT.Exp, scale=-1.0).then_inc(s["cexp"], 1)

                def col(m, b):
                    return mod[:, m, b:b + 1] if isinstance(b, int) else mod[:, m, bass.ds(b, 1)]

                def input_T(b, g, nth):
                    n = GB * b + g
                    wait_all(act, s["mod_ready"], 2, (s["h_ps"], nth),
                             *([(s["scores_ready"], BT * b), (s["ks_ready"], b)] if g == 0 else []))
                    act.activation(ht[:, g, :], ps_h[:, :], ACT.Identity, bias=col(SA, b), scale=col(CA, b))
                    act.activation(hthi[:, g, :], ps_h[:, :], ACT.Identity, bias=col(SA, b),
                                   scale=col(CA, b)).then_inc(s["ht_evac"], 1)

                def keys_hi(b):
                    act.wait_ge(s["ks_ps"], b + 1)
                    act.activation(kthi[:, :], ps_av[:, :], ACT.Copy).then_inc(s["kthi_ready"], 1)

                def exps(b, g, t):
                    i = BT * b + TG * g + t
                    act.wait_ge(s["nmax_ready"], i + 1)
                    if t < 2 and g == 0:
                        act.wait_ge(s["v_split"], 1)
                    act.activation(probs[:, t % 2, :], ps_s[t % 2][:, :], ACT.Exp, bias=nmax[:, g, t:t + 1],
                                   accum_out=rsum[:, g, t:t + 1]).then_inc(s["exp_done"], 1)

                def probs_hi(b, g, t):
                    act.wait_ge(s["pt_ps"], BT * b + TG * g + t + 1)
                    act.activation(sphi[:, g, :, t * P:(t + 1) * P],
                                   ps_pt[t % 2][:, :].rearrange("p (c n) -> p c n", c=KC),
                                   ACT.Copy).then_inc(s["pthi_ready"], 1)

                def att_T(b, g):
                    n = GB * b + g
                    wait_all(act, s["mod_ready"], 2, (s["pv_done"], n + 1), (s["back_ps"], ONE + n))
                    act.activation(att[:, :], ps_av[:, :], ACT.Copy, scale=col(GA, b)).then_inc(s["att_ready"], 1)

                def input2_T(b, g, nth):
                    n = GB * b + g
                    wait_all(act, s["mod_ready"], 2, (s["h_ps"], nth), (s["log_ps"], ONE + n), (s["h2_split"], ONE + n))
                    act.activation(h2[:, :], ps_h[:, :], ACT.Identity, bias=col(SB, b),
                                   scale=col(CB, b)).then_inc(s["h2_ready"], 1)

                def gate_exp(b, g):
                    n = GB * b + g
                    act.wait_ge(s["dlt_ready"], n + 1)
                    act.wait_ge(s["em_ready"], ONE + n)
                    act.activation(ex[:, :, :], dlt[:, :, :], ACT.Exp).then_inc(s["ex_ready"], 1)

                def group(b, g):
                    exps(b, g, 0)
                    exps(b, g, 1)
                    probs_hi(b, g, 0)
                    exps(b, g, 2)
                    probs_hi(b, g, 1)
                    exps(b, g, 3)
                    probs_hi(b, g, 2)
                    probs_hi(b, g, 3)

                def batch(b, last):
                    group(b, 0)
                    att_T(b, 0)
                    group(b, 1)
                    input2_T(b, 0, 4 * b + 3)
                    gate_exp(b, 0)
                    if not last:
                        input_T(b + 1, 0, 4 * b + 4)
                    att_T(b, 1)
                    if not last:
                        input_T(b + 1, 1, 4 * b + 5)
                        keys_hi(b + 1)
                    input2_T(b, 1, 4 * b + (4 if last else 6))
                    gate_exp(b, 1)

                input_T(0, 0, 1)
                input_T(0, 1, 2)
                keys_hi(0)
                with act.Fori(0, B - 1) as b:
                    batch(b, False)
                batch(B - 1, True)

            @block.vector
            def _(dve):
                for name in ("x2_done", "lg_ready", "em_ready", "aggr1", "aggr2", "xhat_ready", "xhat2_ready"):
                    dve.sem_inc(s[name], ONE)
                dve.wait_ge(s["rows_T"], 1)
                dve.tensor_copy(cols[:, :], ps_back[:, 0:E * HC + E + B]).then_inc(s["cols_ready"], 1)
                dve.wait_ge(s["cexp"], 1)
                dve.tensor_scalar(sil[:, 1, :], sil[:, 0, :], 1.0, None, ALU.add).then_inc(s["c1"], 1)
                dve.wait_ge(s["c1"], 1)
                dve.reciprocal(sil[:, 0, :], sil[:, 1, :]).then_inc(s["crec"], 1)
                dve.wait_ge(s["crec"], 1)
                dve.wait_ge(s["cols_ready"], 1)
                dve.tensor_tensor(sil[:, 2, :], cc, sil[:, 0, :], ALU.mult).then_inc(s["sil_ready"], 1)

                def modulation():
                    dve.wait_ge(s["mod_ps"], 1)
                    dve.tensor_copy(mod[:, :, :], ps_log[:, 0:MODS * B].rearrange("p (m b) -> p m b", b=B)).then_inc(s["mod_copied"], 1)
                    dve.wait_ge(s["mod_copied"], 1)
                    dve.tensor_scalar(mod[:, CA, :], mod[:, CA, :], 1.0, None, ALU.add)
                    dve.tensor_scalar(mod[:, CB, :], mod[:, CB, :], 1.0, None, ALU.add)
                    for n, m in enumerate((GA, GBM)):
                        dve.tensor_scalar(gsgn[:, n, 0, :], mod[:, m, :], 0.0, 2.0, ALU.is_ge, ALU.mult).then_inc(s["mod_step"], 1)
                        dve.scalar_tensor_tensor(out=gsgn[:, n, 1, :], in0=mod[:, m, :], scalar=-1.0, in1=mod[:, m, :],
                                                 op0=ALU.mult, op1=ALU.max).then_inc(s["mod_step"], 1)
                        dve.wait_ge(s["mod_step"], 4 * n + 2)
                        dve.tensor_scalar(gsgn[:, n, 0, :], gsgn[:, n, 0, :], -1.0, None, ALU.add).then_inc(s["mod_step"], 1)
                        dve.tensor_scalar(gsgn[:, n, 1, :], gsgn[:, n, 1, :], 0.25, None, ALU.max).then_inc(s["mod_step"], 1)
                        dve.wait_ge(s["mod_step"], 4 * n + 4)
                        dve.tensor_tensor(mod[:, m, :], gsgn[:, n, 0, :], gsgn[:, n, 1, :], ALU.mult).then_inc(s["mod_ready"], 1)
                    dve.wait_ge(s["mod_ready"], 2)
                    for g in range(GB):
                        dve.tensor_copy(gb_g[:, :].rearrange("p (b g) -> p b g", g=GB)[:, :, g], mod[:, GBM, :]).then_inc(s["gb_ready"], 1)

                def tile_of(b, t):
                    return x_sb[:, BT * b + t, :] if isinstance(b, int) else x_sb[:, bass.ds(BT * b + t, 1), :].rearrange("p a d -> p (a d)")

                def normalize(b, g, slot, n, after):
                    stat, aggr, var, rst, xhat = (("stat1", "aggr1", "var1", "rstd1", "xhat_ready"),
                                                  ("stat2", "aggr2", "var2", "rstd2", "xhat2_ready"))[slot]
                    wait_all(dve, x_b[0], 16, (s[aggr], ONE + TG * n),
                             *([(s["x2_done"], ONE + n + 1)] if slot else []))
                    for t in range(TG):
                        dve.bn_stats(st[:, slot, t, :], tile_of(b, TG * g + t)).then_inc(s[stat], 1)
                    wait_all(dve, x_b[0], 16, (s[stat], TG * n + TG), (s[xhat], ONE + n))
                    for t in range(TG):
                        dve.bn_aggr(mv[:, slot, t, :], st[:, slot, t, :]).then_inc(s[aggr], 1)
                    dve.wait_ge(s[aggr], ONE + TG * n + TG)
                    dve.tensor_scalar(veps[:, slot, :], mv[:, slot, :, 1], EPS, None, ALU.add).then_inc(s[var], 1)
                    dve.wait_ge(s[rst], n + 1)
                    dve.wait_ge(*after)
                    for t in range(TG):
                        op = dve.tensor_scalar(xh[:, slot, t, :], tile_of(b, TG * g + t), mv[:, slot, t, 0:1],
                                               rstd[:, slot, t:t + 1], ALU.subtract, ALU.mult)
                    op.then_inc(s[xhat], 1)

                def input_lo(b, g):
                    dve.wait_ge(s["ht_evac"], GB * b + g + 1)
                    dve.tensor_tensor(htlo[:, g, :], ht[:, g, :], hthi[:, g, :].bitcast(F32),
                                      ALU.subtract).then_inc(s["ht_split"], 1)

                def scale_keys(b):
                    if isinstance(b, int):
                        dve.wait_ge(k_in, 16)
                    for j in range(KC):
                        g, at = divmod(STEP * j, GT)
                        op = dve.tensor_scalar(ks[:, j, :], k_sb[:, j, :], ht[:, g, at:at + 1], None, ALU.mult)
                    op.then_inc(s["ks_ready"], 1)

                def keys_lo(b):
                    dve.wait_ge(s["kthi_ready"], b + 1)
                    dve.tensor_tensor(ktlo[:, :], ps_av[:, :], kthi[:, :].bitcast(F32), ALU.subtract).then_inc(s["kt_ready"], 1)

                def maxima(b, g, t):
                    dve.wait_ge(s["scores_ready"], BT * b + TG * g + t + 1)
                    dve.tensor_reduce(nmax[:, g, t:t + 1], ps_s[t % 2][:, :], AX_X, ALU.max,
                                      negate=True).then_inc(s["nmax_ready"], 1)

                def probs_lo(b, g, t):
                    dve.wait_ge(s["pthi_ready"], BT * b + TG * g + t + 1)
                    at = slice(t * P, (t + 1) * P)
                    dve.tensor_tensor(splo[:, g, :, at], ps_pt[t % 2][:, :].rearrange("p (c n) -> p c n", c=KC),
                                      sphi[:, g, :, at].bitcast(F32), ALU.subtract).then_inc(s["pt_split"], 1)

                def residual(b, g):
                    n = GB * b + g
                    dve.wait_ge(s["exp_done"], TG * (n + 1))
                    dve.reciprocal(rinv[:, :], rsum[:, g, :]).then_inc(s["rinv_ready"], 1)
                    dve.wait_ge(s["back_ps"], ONE + n + 1)
                    dve.wait_ge(s["rinv_ready"], n + 1)
                    for t in range(TG):
                        xt = tile_of(b, TG * g + t)
                        op = dve.scalar_tensor_tensor(out=xt, in0=ps_back[:, t * P:(t + 1) * P], scalar=rinv[:, t:t + 1],
                                                      in1=xt, op0=ALU.mult, op1=ALU.add)
                    op.then_inc(s["x2_done"], 1)

                def gate_logits(b, g):
                    n = GB * b + g
                    dve.wait_ge(s["log_ps"], ONE + n + 1)
                    dve.wait_ge(router_in, 32)
                    dve.tensor_tensor(lg[:, :, :], ps_log[:, 0:TG * E].rearrange("p (t e) -> p t e", e=E),
                                      br_sb[:, :].unsqueeze(1).to_broadcast([P, TG, E]), ALU.add).then_inc(s["lg_ready"], 1)
                    wait_all(dve, router_in, 32, (s["lg_ready"], ONE + n + 1))
                    for t in range(TG):
                        op = dve.max(top[:, t, :], lg[:, t, :])
                    op.then_inc(s["top_ready"], 1)
                    dve.wait_ge(s["top_ready"], n + 1)
                    dve.tensor_tensor(dlt[:, :, :], lg[:, :, :], top[:, :, 0:1].to_broadcast([P, TG, E]),
                                      ALU.subtract).then_inc(s["dlt_ready"], 1)
                    dve.tensor_tensor(keep[:, :, :], lg[:, :, :], top[:, :, 1:2].to_broadcast([P, TG, E]),
                                      ALU.is_ge).then_inc(s["keep_ready"], 1)

                def gate_weights(b, g):
                    n = GB * b + g
                    dve.wait_ge(s["ex_ready"], n + 1)
                    dve.wait_ge(s["keep_ready"], n + 1)
                    dve.tensor_tensor(em[:, :, :], ex[:, :, :], keep[:, :, :], ALU.mult).then_inc(s["em_ready"], 1)
                    dve.wait_ge(s["em_ready"], ONE + n + 1)
                    dve.tensor_reduce(esum[:, :], em[:, :, :], AX_X, ALU.add).then_inc(s["esum_ready"], 1)
                    dve.wait_ge(s["esum_ready"], n + 1)
                    dve.reciprocal(einv[:, :], esum[:, :]).then_inc(s["einv_ready"], 1)
                    dve.wait_ge(s["einv_ready"], n + 1)
                    dve.tensor_tensor(wgt[:, :, :], em[:, :, :], einv[:, :].unsqueeze(2).to_broadcast([P, TG, E]),
                                      ALU.mult).then_inc(s["wgt_ready"], 1)
                    dve.wait_ge(s["wgt_ready"], n + 1)
                    if isinstance(n, int):
                        gt = gates[:, n, :]
                    else:
                        gt = gates[:, bass.ds(n, 1), :].rearrange("p a w -> p (a w)")
                    gt = gt.rearrange("p (t w) -> p t w", w=WROWS)
                    dve.tensor_copy(gt[:, :, 0:E].bitcast(F32R), wgt[:, :, :]).then_inc(s["gate_hi"], 1)
                    dve.wait_ge(s["gate_hi"], n + 1)
                    dve.tensor_tensor(gt[:, :, E:WROWS].bitcast(F32R), wgt[:, :, :], gt[:, :, 0:E],
                                      ALU.subtract).then_inc(s["gates_ready"], 1)

                def group(b, g, between=None):
                    maxima(b, g, 0)
                    maxima(b, g, 1)
                    probs_lo(b, g, 0)
                    if between:
                        residual(b, 0)
                        normalize(b, 0, 1, GB * b, (s["h_ps"], 4 * b + 2))
                    maxima(b, g, 2)
                    probs_lo(b, g, 1)
                    maxima(b, g, 3)
                    probs_lo(b, g, 2)
                    probs_lo(b, g, 3)
                    if between:
                        gate_logits(b, 0)

                def batch(b, last):
                    group(b, 0)
                    group(b, 1, True)
                    if not last:
                        if isinstance(b, int):
                            dve.wait_ge(x_b[b + 1], 16)
                        normalize(b + 1, 0, 0, GB * (b + 1), (s["h_ps"], 4 * b + 2))
                        normalize(b + 1, 1, 0, GB * (b + 1) + 1, (s["h_ps"], 4 * b + 4))
                    gate_weights(b, 0)
                    if not last:
                        input_lo(b + 1, 0)
                    residual(b, 1)
                    normalize(b, 1, 1, GB * b + 1, (s["h_ps"], 4 * b + 3))
                    if not last:
                        input_lo(b + 1, 1)
                        scale_keys(b + 1)
                        keys_lo(b + 1)
                    gate_logits(b, 1)
                    gate_weights(b, 1)

                dve.wait_ge(x_b[0], 16)
                normalize(0, 0, 0, 0, (s["h_ps"], 0))
                modulation()
                normalize(0, 1, 0, 1, (s["h_ps"], 1))
                input_lo(0, 0)
                input_lo(0, 1)
                scale_keys(0)
                keys_lo(0)
                dve.wait_ge(v_in, 16)
                dve.tensor_copy(vhi[:, :, :], v_raw).then_inc(s["v_hi"], 1)
                dve.wait_ge(s["v_hi"], 1)
                dve.tensor_tensor(vlo[:, :, :], v_raw, vhi[:, :, :].bitcast(F32), ALU.subtract).then_inc(s["v_split"], 1)
                for i in range(1, B):
                    dve.wait_ge(x_b[i], 16)
                with dve.Fori(0, B - 1) as b:
                    batch(b, False)
                batch(B - 1, True)

        names = """u_ready gel_ready sp_hi sp_ready o_ready gb_ps gbc_ready
            gated added outT_done fin_ps y_done out_done sel_zeroed sel_one sel_ready gcur_ready
            gT_ps gT_ready""".split()
        m = {n: sem("moe_" + n) for n in names}
        HB = HC // 2
        with nc.Block() as block:

            def group_cols(t, g):
                return t[:, g * GT:(g + 1) * GT] if isinstance(g, int) else t[:, bass.ts(g, GT)]

            @block.sync
            def _(sp):
                def store(g):
                    sp.wait_ge(m["y_done"], ONE + g + 1)
                    at = slice(g * TG, (g + 1) * TG) if isinstance(g, int) else bass.ts(g, TG)
                    sp.dma_start(out_dram[:, at, :], x_sb[:, at, :]).then_inc(m["out_done"], 16)

                with sp.Fori(0, NG) as g:
                    store(g)
                sp.wait_ge(m["out_done"], 16 * NG)

            @block.gpsimd
            def _(pool):
                def take_gates(g):
                    pool.wait_ge(m["gT_ps"], g)
                    src = gates[:, g, :] if isinstance(g, int) else gates[:, bass.ds(g, 1), :].rearrange("p a w -> p (a w)")
                    pool.tensor_copy(gcur[:, :], src).then_inc(m["gcur_ready"], 1)

                pool.sem_inc(m["added"], ONE)
                take_gates(0)
                for h in range(2):
                    pool.memset(sel32, 0.0).then_inc(m["sel_zeroed"], 1)
                    pool.wait_ge(m["sel_zeroed"], h + 1)
                    sv = sel32.rearrange("p (e n) -> p e n", n=P)
                    for part in range(2):
                        pool.affine_select(out=sv, in_=sv, compare_op=ALU.not_equal, fill=1.0,
                                           base=-(E * part + KC * h), pattern=[[-1, KC], [0, P]],
                                           channel_multiplier=1).then_inc(m["sel_one"], 1)
                        pool.wait_ge(m["sel_one"], 2 * h + part + 1)
                    pool.tensor_copy(sel[:, KC * h:KC * (h + 1), :], sv).then_inc(m["sel_ready"], 1)
                    pool.wait_ge(m["sel_ready"], h + 1)

                def add(g, e):
                    pool.wait_ge(m["gated"], ONE + E * g + e + 1)
                    pool.tensor_tensor(acc, acc, msk[:, e % 2, :], ALU.add).then_inc(m["added"], 1)
                    pool.wait_ge(m["added"], ONE + (E - 1) * g + e)

                with pool.Fori(0, NG - 1) as g:
                    for e in range(1, E):
                        add(g, e)
                        if e == 1:
                            take_gates(g + 1)
                for e in range(1, E):
                    add(NG - 1, e)

            @block.tensor
            def _(pe):
                def up(g, e):
                    for j in range(HC):
                        if not (isinstance(g, int) and g == e == 0):
                            pe.wait_ge(m["gel_ready"], HC * (E * g + e - 1) + j + 1)
                        w = slice(j * P, (j + 1) * P)
                        pe.matmul(ps_u[j][:, :], w1lo[:, e, w], group_cols(h2hi, g), start=True, stop=False)
                        pe.matmul(ps_u[j][:, :], w1hi[:, e, w], group_cols(h2lo, g), start=False, stop=False)
                        pe.matmul(ps_u[j][:, :], w1hi[:, e, w], group_cols(h2hi, g), start=False, stop=True).then_inc(m["u_ready"], 1)

                def spread(g, e):
                    i = E * g + e
                    pe.wait_ge(m["gT_ready"], g + 1)
                    pe.wait_ge(m["gbc_ready"], i)
                    pe.matmul(ps_gb[:, :], sel[:, e, :], gT, start=True, stop=True).then_inc(m["gb_ps"], 1)

                def down(g, e):
                    i = E * g + e
                    if not (isinstance(g, int) and g == e == 0):
                        pe.wait_ge(m["gated"], ONE + i - 1)
                    mm = None
                    for j in range(HC):
                        if j % HB == 0:
                            pe.wait_ge(m["sp_ready"], 2 * i + j // HB + 1)
                        w, at = slice(j * P, (j + 1) * P), e % 2
                        pe.matmul(ps_o[at][:, :], w2lo[:, e, w], sphi[:, at, j, :], start=(j == 0), stop=False)
                        pe.matmul(ps_o[at][:, :], w2hi[:, e, w], splo[:, at, j, :], start=False, stop=False)
                        mm = pe.matmul(ps_o[at][:, :], w2hi[:, e, w], sphi[:, at, j, :], start=False, stop=(j == HC - 1))
                    mm.then_inc(m["o_ready"], 1)

                def turn_gates(g):
                    pe.wait_ge(m["gcur_ready"], g + 1)
                    if not (isinstance(g, int) and g == 0):
                        pe.wait_ge(m["y_done"], ONE + g - 1)
                    for t in range(TG):
                        mm = pe.transpose(ps_x[0:WROWS, t * P:(t + 1) * P], gcur[:, t * WROWS:(t + 1) * WROWS], ident[:, :])
                    mm.then_inc(m["gT_ps"], 1)

                def turn_out(g, last):
                    pe.wait_ge(m["outT_done"], g + 1)
                    if not last:
                        pe.wait_ge(m["gT_ready"], g + 2)
                    for t in range(TG):
                        mm = pe.transpose(ps_x[:, t * P:(t + 1) * P], outT[:, t * P:(t + 1) * P], ident[:, :])
                    mm.then_inc(m["fin_ps"], 1)

                pe.sem_inc(m["fin_ps"], ONE)
                pe.wait_ge(m["sel_ready"], 2)
                turn_gates(0)
                up(0, 0)
                up(0, 1)
                spread(0, 0)
                down(0, 0)
                with pe.Fori(0, NG - 1) as g:
                    for e in range(1, E):
                        spread(g, e)
                        if e < E - 1:
                            up(g, e + 1)
                        else:
                            up(g + 1, 0)
                            turn_gates(g + 1)
                        down(g, e)
                    up(g + 1, 1)
                    turn_out(g, False)
                    spread(g + 1, 0)
                    down(g + 1, 0)
                for e in range(1, E):
                    spread(NG - 1, e)
                    if e < E - 1:
                        up(NG - 1, e + 1)
                    down(NG - 1, e)
                turn_out(NG - 1, True)

            @block.scalar
            def _(act):
                def gelus(g, e):
                    i = E * g + e
                    for j in range(HC):
                        act.wait_ge(m["u_ready"], HC * i + j + 1)
                        if j % HB == 0 and not (isinstance(g, int) and g == 0 and e < 2):
                            act.wait_ge(m["sp_ready"], 2 * (i - 2) + j // HB + 1)
                        n = e * HC + j
                        act.activation(gel[:, e % 2, j, :], ps_u[j][:, :], ACT.Gelu,
                                       bias=b1c[:, n:n + 1]).then_inc(m["gel_ready"], 1)

                def gate_out(g, e):
                    i = E * g + e
                    act.wait_ge(m["gb_ps"], i + 1)
                    if not (isinstance(g, int) and g == e == 0):
                        act.wait_ge(m["gated"], ONE + i - 1)
                    act.activation(gbc[:, e % 2, :], ps_gb[:, :], ACT.Copy).then_inc(m["gbc_ready"], 1)

                def gates_T(g):
                    act.wait_ge(m["gT_ps"], g + 1)
                    act.wait_ge(m["gb_ps"], E * g)
                    act.activation(gT, ps_x[0:WROWS, :], ACT.Copy).then_inc(m["gT_ready"], 1)

                def scale_out(g):
                    wait_all(act, s["gb_ready"], GB, (m["added"], ONE + (E - 1) * (g + 1)), (m["fin_ps"], ONE + g))
                    gcol = gb_g[:, g:g + 1] if isinstance(g, int) else gb_g[:, bass.ds(g, 1)]
                    act.activation(outT[:, :], acc, ACT.Copy, scale=gcol).then_inc(m["outT_done"], 1)

                gates_T(0)
                gelus(0, 0)
                gelus(0, 1)
                gate_out(0, 0)
                with act.Fori(0, NG - 1) as g:
                    for e in range(1, E):
                        gate_out(g, e)
                        if e < E - 1:
                            gelus(g, e + 1)
                        else:
                            gelus(g + 1, 0)
                            gates_T(g + 1)
                    scale_out(g)
                    gelus(g + 1, 1)
                    gate_out(g + 1, 0)
                for e in range(1, E):
                    gate_out(NG - 1, e)
                    if e < E - 1:
                        gelus(NG - 1, e + 1)
                scale_out(NG - 1)

            @block.vector
            def _(dve):
                def split(g, e):
                    i = E * g + e
                    for half in range(2):
                        c = slice(half * HB, (half + 1) * HB)
                        dve.wait_ge(m["gel_ready"], HC * i + (half + 1) * HB)
                        dve.tensor_copy(sphi[:, e % 2, c, :], gel[:, e % 2, c, :]).then_inc(m["sp_hi"], 1)
                        dve.wait_ge(m["sp_hi"], 2 * i + half + 1)
                        dve.tensor_tensor(splo[:, e % 2, c, :], gel[:, e % 2, c, :], sphi[:, e % 2, c, :].bitcast(F32),
                                          ALU.subtract).then_inc(m["sp_ready"], 1)

                def gate(g, e):
                    i = E * g + e
                    dve.wait_ge(m["o_ready"], i + 1)
                    dve.wait_ge(m["gbc_ready"], i + 1)
                    if e == 0:
                        dve.wait_ge(m["outT_done"], g)
                    else:
                        dve.wait_ge(m["added"], ONE + (E - 1) * g + max(e - 2, 0))
                    dve.scalar_tensor_tensor(out=acc if e == 0 else msk[:, e % 2, :], in0=ps_o[e % 2][:, :],
                                             scalar=b2c[:, e:e + 1], in1=gbc[:, e % 2, :],
                                             op0=ALU.add, op1=ALU.mult).then_inc(m["gated"], 1)

                def finish(g):
                    dve.wait_ge(m["fin_ps"], ONE + g + 1)
                    at = slice(g * TG, (g + 1) * TG) if isinstance(g, int) else bass.ts(g, TG)
                    dve.tensor_tensor(x_sb[:, at, :], ps_x[:, :].rearrange("p (t d) -> p t d", d=D), x_sb[:, at, :],
                                      ALU.add).then_inc(m["y_done"], 1)

                dve.sem_inc(m["gated"], ONE)
                dve.sem_inc(m["y_done"], ONE)
                split(0, 0)
                split(0, 1)
                gate(0, 0)
                with dve.Fori(0, NG - 1) as g:
                    for e in range(1, E):
                        if e < E - 1:
                            split(g, e + 1)
                        else:
                            split(g + 1, 0)
                        gate(g, e)
                    split(g + 1, 1)
                    finish(g)
                    gate(g + 1, 0)
                for e in range(1, E):
                    if e < E - 1:
                        split(NG - 1, e + 1)
                    gate(NG - 1, e)
                finish(NG - 1)


_INS = ['L0_attn_q', 'L0_attn_k', 'L0_attn_v', 'L0_ffn_W1', 'L0_ffn_b1', 'L0_ffn_W2', 'L0_ffn_b2',
        'L0_ffn_Wr', 'L0_ffn_br', 'L0_c', 'L0_wmod']


def kernel(**inputs):
    import numpy as _np
    import concourse.bacc as _bacc
    from concourse import mybir as _mybir
    from concourse.bass_utils import run_bass_kernel_spmd as _run

    nc = _bacc.Bacc("TRN2", target_bir_lowering=False, num_devices=1)
    arrays, args = {}, []
    for name in _INS:
        a = _np.ascontiguousarray(inputs[name])
        arrays[f"in_{name}_dram"] = a
        args.append(nc.dram_tensor(f"in_{name}_dram", a.shape, _mybir.dt.from_np(a.dtype), kind="ExternalInput").ap())
    out = nc.dram_tensor("out_0_dram", inputs['L0_attn_q'].shape, _mybir.dt.float32, kind="ExternalOutput").ap()
    adaln_block(nc, *args, out)
    r = _run(nc, [arrays], core_ids=[0])
    return r.results[0]["out_0_dram"]
```

```python
from contextlib import ExitStack

import concourse.bass as bass
from concourse import mybir

ALU = mybir.AluOpType
ACT = mybir.ActivationFunctionType
F32 = mybir.dt.float32
F32R = mybir.dt.float32r
AX_X = mybir.AxisListType.X

P = 128
TG = 4
GT = TG * P
SPLIT = 2


def adaln_block(nc, q, k, v, W1, b1, W2, b2, Wr, br, c, wmod, out):
    B, S, D = q.shape
    T = k.shape[1]
    E, _, H = W1.shape
    MODS = wmod.shape[1] // D
    KC = T // P
    HC = H // P
    NT = B * S // P
    NG = NT // TG
    GB = NG // B
    STEP = S // 4
    EPS = 1e-5
    WROWS = 2 * E
    R = E * HC + E + B
    EW = 2
    WCH = E // EW
    SA, CA, GA, SB, CB, GBM = range(6)
    assert D == P and T == GT and GB == 2 and MODS == 6 and KC == 4 and HC == 4 and E == 8

    with ExitStack() as ctx:
        def sb(name, shape, dt=F32):
            return ctx.enter_context(nc.sbuf_tensor(name, shape, dt))

        def sem(name):
            return ctx.enter_context(nc.semaphore(name))

        x_sb = sb("x_sb", [P, NT, D])
        w1hi = sb("w1hi", [P, E, H], F32R)
        w1lo = sb("w1lo", [P, E, H], F32R)
        w2hi = sb("w2hi", [P, E, HC * D], F32R)
        w2lo = sb("w2lo", [P, E, HC * D], F32R)
        wraw = sb("wraw", [P, 2, EW * H])
        h2hi = sb("h2hi", [P, NT * P], F32R)
        h2lo = sb("h2lo", [P, NT * P], F32R)
        gel = sb("gel", [P, 2, HC, GT])
        sphi = sb("sphi", [P, 2, HC, GT], F32R)
        splo = sb("splo", [P, 2, HC, GT], F32R)
        pt = gel[:, 0, :, :]
        wm_sb = gel[:, 0, 0:2, :].rearrange("p a b -> p (a b)")[:, 0:MODS * D]
        ks = gel[:, 1, :, :].rearrange("p b (n d) -> p b n d", d=D)
        kT = sb("kT", [P, B * T])
        k_sb = sb("k_sb", [P, KC, D])
        v_sb = sb("v_sb", [P, KC, D])
        probs = sb("probs", [P, 2, T])
        att = sb("att", [P, GT])
        xh = sb("xh", [P, 2, TG, D])
        ht = sb("ht", [P, GT])
        h2 = sb("h2", [P, GT])
        ident = sb("ident", [P, P])
        rows = att[0:R, 0:P]
        cols = sb("cols", [P, R])
        sil = sb("sil", [P, 3, B])
        mod = sb("mod", [P, MODS, B])
        gsgn = sb("gsgn", [P, 2, 2, B])
        mod_g = sb("mod_g", [P, MODS, NG])
        xk = sb("xk", [B * KC, D])
        xkh = sb("xkh", [B * KC, D])
        kst = sb("kst", [B * KC, 6])
        kmv = sb("kmv", [B * KC, 4])
        kfac = sb("kfac", [P, B, KC])
        wr_sb = sb("wr_sb", [P, E])
        br_sb = sb("br_sb", [P, E])
        st = sb("st", [P, 2, TG, 6])
        mv = sb("mv", [P, 2, TG, 2])
        veps = sb("veps", [P, 2, TG])
        rstd = sb("rstd", [P, 2, TG])
        mhalf = sb("mhalf", [P, TG])
        nmax = sb("nmax", [P, TG])
        rsum = sb("rsum", [P, TG])
        rinv = sb("rinv", [P, TG])
        lg = sb("lg", [P, TG, E])
        top = sb("top", [P, TG, 8])
        dlt = sb("dlt", [P, TG, E])
        keep = sb("keep", [P, TG, E])
        ex = sb("ex", [P, TG, E])
        em = sb("em", [P, TG, E])
        esum = sb("esum", [P, TG])
        einv = sb("einv", [P, TG])
        wgt = sb("wgt", [P, TG, E])
        gates = sb("gates", [P, NG, TG * WROWS])
        gcur = sb("gcur", [P, TG * WROWS])
        sel = sb("sel", [WROWS, E, P], F32R)
        gT = sb("gT", [WROWS, GT], F32R)[:, :]
        b1c = cols[:, 0:E * HC]
        b2c = cols[:, E * HC:E * HC + E]
        cc = cols[:, E * HC + E:R]
        gbc = probs
        msk = wraw[:, 0, :].rearrange("p (s t) -> p s t", s=2)
        acc = wraw[:, 1, 0:GT]
        outT = att

        ps = [ctx.enter_context(nc.psum_tensor(f"ps{i}", [P, GT], F32)) for i in range(8)]
        ps_s, ps_pt, ps_av, ps_back, ps_h, ps_log = ps[0:2], ps[2:4], ps[4], ps[5], ps[6], ps[7]
        ps_k = ps[2:6]
        ps_u, ps_o, ps_gb, ps_x = ps[0:4], ps[4:6], ps[6], ps[7]

        ONE = 1

        rows_in, xk_in, wm_in, k_in, v_in, router_in = map(sem, (
            "rows_in", "xk_in", "wm_in", "k_in", "v_in", "router_in"))
        x_in = [sem(f"x_in{i}") for i in range(B)]
        w_in = [sem(f"w_in{i}") for i in range(2 * WCH)]
        names = """zeroed ident_ready sel_ready rows_T cols_ready cexp c1 crec sil_ready mod_ps mod_copied
            mod_ready mod_step modg_ready k_stat k_aggr k_var k_rstd xkh_ready kfac_ps kfac_ready ks_ready ks_ps
            kT_ready w_hi w_split stat1 aggr1 var1 rstd1 xhat1 ht_ps ht_ready
            scores_ready nmax_ready exp_done pt_ps pt_ready pv_done att_ready
            back_ps x2_done rinv_ready stat2 aggr2 var2 rstd2 xhat2 h2_ps h2_ready h2_split
            log_ps lg_ready top_ready dlt_ready keep_ready ex_ready em_ready esum_ready einv_ready
            wgt_ready gate_hi gates_ready""".split()
        s = {n: sem(n) for n in names}
        names = """u_ready gel_ready sp_hi sp_ready o_ready gb_ps gbc_ready gated added outT_done
            fin_ps y_done out_done gcur_ready gT_ps gT_ready""".split()
        m = {n: sem("moe_" + n) for n in names}

        x_dram = q.rearrange("b s d -> (b s) d").rearrange("(n p) d -> p n d", p=P)
        xk_dram = q.rearrange("b (j r) d -> (b j) r d", r=STEP)[:, 0, :]
        out_dram = out.rearrange("b s d -> (b s) d").rearrange("(n p) d -> p n d", p=P)
        k_dram = k[0].rearrange("(n p) d -> p n d", p=P)
        v_dram = v[0].rearrange("(n p) d -> p n d", p=P)
        w1_dram = W1.rearrange("e d h -> d e h")
        w2_dram = W2.rearrange("e (c p) d -> p e c d", p=P)
        whi = [w1hi[:, EW * i:EW * (i + 1), :] for i in range(WCH)] + [w2hi[:, EW * i:EW * (i + 1), :] for i in range(WCH)]
        wlo = [w1lo[:, EW * i:EW * (i + 1), :] for i in range(WCH)] + [w2lo[:, EW * i:EW * (i + 1), :] for i in range(WCH)]
        W_SLOT = {0: (0, 1), 1: (2, 3), NG - 1: (4, 5), NG: (6, 7)}

        def wait_all(eng, loaded, value, *counted):
            counted = [(of, n if isinstance(n, int) else eng.to_reg(n)) for of, n in counted]
            eng.wait_ge(loaded, value)
            for of, n in counted:
                eng.wait_ge(of, n)

        def group_cols(t, g):
            return t[:, g * GT:(g + 1) * GT] if isinstance(g, int) else t[:, bass.ts(g, GT)]

        def group_tiles(g):
            return slice(g * TG, (g + 1) * TG) if isinstance(g, int) else bass.ts(g, TG)

        def row_of(t, g):
            return t[:, g, :] if isinstance(g, int) else t[:, bass.ds(g, 1), :].rearrange("p a w -> p (a w)")

        def col_of(mo, g):
            return mod_g[:, mo, g:g + 1] if isinstance(g, int) else mod_g[:, mo, bass.ds(g, 1)]

        def slots(eng, slot):
            slot(0)
            slot(1)
            with eng.Fori(2, NG - 1) as n:
                slot(n)
            slot(NG - 1)
            slot(NG)

        def has(n, group):
            return not isinstance(n, int) or 0 <= group < NG

        with nc.Block() as block:

            @block.sync
            def _(sp):
                sp.dma_start(rows[0:E * HC, :], b1.rearrange("e (c p) -> (e c) p", p=P)).then_inc(rows_in, 16)
                sp.dma_start(rows[E * HC:E * HC + E, :], b2).then_inc(rows_in, 16)
                sp.dma_start(rows[E * HC + E:R, :], c).then_inc(rows_in, 16)
                for i in range(B):
                    t = slice(NT // B * i, NT // B * (i + 1))
                    sp.dma_start(x_sb[:, t, :], x_dram[:, t, :]).then_inc(x_in[i], 16)
                for i in range(2 * WCH):
                    if i >= 2:
                        sp.wait_ge(s["w_split"], i - 1)
                    e0 = EW * (i % WCH)
                    dst = wraw[:, i % 2, :]
                    if i < WCH:
                        sp.dma_start(dst.rearrange("p (e h) -> p e h", h=H), w1_dram[:, e0:e0 + EW, :]).then_inc(w_in[i], 16)
                    else:
                        for j in range(EW):
                            sp.dma_start(dst[:, j * H:(j + 1) * H].rearrange("p (c d) -> p c d", c=HC),
                                         w2_dram[:, e0 + j, :, :]).then_inc(w_in[i], 16)

                def store(g):
                    sp.wait_ge(m["y_done"], ONE + g + 1)
                    sp.dma_start(out_dram[:, group_tiles(g), :], x_sb[:, group_tiles(g), :]).then_inc(m["out_done"], 16)

                with sp.Fori(0, NG) as g:
                    store(g)
                sp.wait_ge(m["out_done"], 16 * NG)

            @block.gpsimd
            def _(pool):
                pool.sem_inc(s["h2_split"], ONE)
                pool.sem_inc(m["added"], ONE)
                pool.memset(mhalf[:, :], -0.5).then_inc(s["zeroed"], 1)
                pool.memset(ident[:, :], 0.0).then_inc(s["zeroed"], 1)
                pool.memset(sel[:, :, :].bitcast(F32), 0.0).then_inc(s["zeroed"], 1)
                pool.wait_ge(s["zeroed"], 3)
                pool.affine_select(out=ident[:, :], in_=ident[:, :], compare_op=ALU.not_equal, fill=1.0,
                                   base=0, pattern=[[-1, P]], channel_multiplier=1).then_inc(s["ident_ready"], 1)
                for part in range(2):
                    pool.affine_select(out=sel[:, :, :], in_=sel[:, :, :].bitcast(F32), compare_op=ALU.not_equal,
                                       fill=1.0, base=-E * part, pattern=[[-1, E], [0, P]],
                                       channel_multiplier=1).then_inc(s["sel_ready"], 1)
                    pool.wait_ge(s["sel_ready"], part + 1)
                pool.wait_ge(s["k_var"], 1)
                pool.tensor_tensor(kmv[:, 3:4], kmv[:, 2:3], mhalf[0:B * KC, 0:1], ALU.pow).then_inc(s["k_rstd"], 1)

                def root(which, n):
                    pool.wait_ge(s[f"var{which}"], n + 1)
                    pool.tensor_tensor(rstd[:, which - 1, :], veps[:, which - 1, :], mhalf[:, :],
                                       ALU.pow).then_inc(s[f"rstd{which}"], 1)

                def slot(n):
                    if has(n, n + 1):
                        root(1, n + 1)
                    if has(n, n - 2):
                        g = n - 2
                        pool.wait_ge(s["h2_ready"], g + 1)
                        pool.tensor_tensor(group_cols(h2lo, g), h2[:, :], group_cols(h2hi, g).bitcast(F32),
                                           ALU.subtract).then_inc(s["h2_split"], 1)
                    if has(n, n - 1):
                        root(2, n - 1)
                    if isinstance(n, int):
                        for i in W_SLOT.get(n, ()):
                            pool.wait_ge(s["w_hi"], i + 1)
                            pool.tensor_tensor(wlo[i], wraw[:, i % 2, :].rearrange("p (e h) -> p e h", e=EW),
                                               whi[i].bitcast(F32), ALU.subtract).then_inc(s["w_split"], 1)

                root(1, 0)
                slots(pool, slot)
                slot(NG + 1)

                def take_gates(g):
                    pool.wait_ge(s["gates_ready"], g + 1)
                    if not (isinstance(g, int) and g == 0):
                        pool.wait_ge(m["gT_ps"], g)
                    pool.tensor_copy(gcur[:, :], row_of(gates, g)).then_inc(m["gcur_ready"], 1)

                take_gates(0)

                def add(g, e):
                    pool.wait_ge(m["gated"], ONE + E * g + e + 1)
                    pool.tensor_tensor(acc, acc, msk[:, e % 2, :], ALU.add).then_inc(m["added"], 1)
                    pool.wait_ge(m["added"], ONE + (E - 1) * g + e)

                with pool.Fori(0, NG - 1) as g:
                    for e in range(1, E):
                        add(g, e)
                        if e == 1:
                            take_gates(g + 1)
                for e in range(1, E):
                    add(NG - 1, e)

            @block.tensor
            def _(pe):
                for name in ("h2_ps", "log_ps"):
                    pe.sem_inc(s[name], ONE)
                pe.sem_inc(m["fin_ps"], ONE)
                pe.wait_ge(s["ident_ready"], 1)
                pe.wait_ge(rows_in, 48)
                pe.transpose(ps_s[0][:, 0:R], rows, ident[0:R, 0:R]).then_inc(s["rows_T"], 1)
                pe.wait_ge(s["xkh_ready"], 1)
                pe.transpose(ps_s[1][:, 0:B * KC], xkh[:, :], ident[0:B * KC, 0:B * KC]).then_inc(s["kfac_ps"], 1)
                pe.wait_ge(s["sil_ready"], 1)
                pe.wait_ge(wm_in, 16)
                for mo in range(MODS):
                    mm = pe.matmul(ps_log[:, mo * B:(mo + 1) * B], wm_sb[:, mo * D:(mo + 1) * D], sil[:, 2, :],
                                   start=True, stop=True)
                mm.then_inc(s["mod_ps"], 1)

                def turn(to, of):
                    for t in range(TG):
                        mm = pe.transpose(to[:, t * P:(t + 1) * P], of[:, t, :], ident[:, :])
                    return mm

                def turn_input(n):
                    pe.wait_ge(s["xhat1"], n + 1)
                    if isinstance(n, int) and n < 3:
                        pe.wait_ge(s["ht_ready"], n)
                    else:
                        pe.wait_ge(s["h2_ready"], n - 2)
                    turn(ps_h, xh[:, 0, :, :]).then_inc(s["ht_ps"], 1)

                def scores(n, t):
                    if t == 0:
                        pe.wait_ge(s["ht_ready"], n + 1)
                    pe.matmul(ps_s[t % 2][:, :], ht[:, t * P:(t + 1) * P], group_cols(kT, n // 2 if isinstance(n, int) else n >> 1),
                              start=True, stop=True).then_inc(s["scores_ready"], 1)

                def turn_probs(n, t):
                    pe.wait_ge(s["exp_done"], TG * n + t + 1)
                    if t >= 2:
                        pe.wait_ge(s["pt_ready"], TG * n + t - 1)
                    turn(ps_pt[t % 2], probs[:, t % 2, :].rearrange("p (c n) -> p c n", c=KC)).then_inc(s["pt_ps"], 1)

                def sums(n):
                    pe.wait_ge(s["pt_ready"], TG * (n + 1))
                    if not (isinstance(n, int) and n == 0):
                        pe.wait_ge(s["att_ready"], n)
                    for j in range(KC):
                        mm = pe.matmul(ps_av[:, :], v_sb[:, j, :], pt[:, j, :], start=(j == 0), stop=(j == KC - 1))
                    mm.then_inc(s["pv_done"], 1)

                def turn_sums(n):
                    pe.wait_ge(s["att_ready"], n + 1)
                    if not (isinstance(n, int) and n == 0):
                        pe.wait_ge(s["x2_done"], n)
                    turn(ps_back, att[:, :].rearrange("p (t n) -> p t n", t=TG)).then_inc(s["back_ps"], 1)

                def turn_input2(n, read):
                    pe.wait_ge(s["xhat2"], n + 1)
                    pe.wait_ge(*read)
                    turn(ps_h, xh[:, 1, :, :]).then_inc(s["h2_ps"], 1)

                def logits(n):
                    pe.wait_ge(s["h2_ready"], n + 1)
                    pe.wait_ge(s["lg_ready"], ONE + n)
                    for t in range(TG):
                        mm = pe.matmul(ps_log[:, t * E:(t + 1) * E], h2[:, t * P:(t + 1) * P], wr_sb[:, :],
                                       start=True, stop=True)
                    mm.then_inc(s["log_ps"], 1)

                def slot(n):
                    group, before, before2, after = (has(n, n + i) for i in (0, -1, -2, 1))
                    if group:
                        scores(n, 0)
                        scores(n, 1)
                    if before:
                        sums(n - 1)
                    if before2:
                        turn_input2(n - 2, (s["ht_ready"], n + 1) if group else (s["ht_ready"], NG) if before else (s["h2_ready"], NG - 1))
                    if group:
                        turn_probs(n, 0)
                        scores(n, 2)
                        turn_probs(n, 1)
                        scores(n, 3)
                    if before:
                        turn_sums(n - 1)
                    if before2:
                        logits(n - 2)
                    if group:
                        turn_probs(n, 2)
                    if after:
                        turn_input(n + 1)
                    if group:
                        turn_probs(n, 3)

                turn_input(0)
                for b in range(B):
                    pe.wait_ge(s["ks_ready"], b + 1)
                    turn(ps_k[b], ks[:, b, :, :]).then_inc(s["ks_ps"], 1)
                pe.wait_ge(v_in, 16)
                pe.wait_ge(router_in, 32)
                pe.wait_ge(s["kT_ready"], B)
                slots(pe, slot)

                HB = HC // 2

                def up(g, e):
                    if isinstance(g, int) and g == 0 and e % EW == 0:
                        pe.wait_ge(s["w_split"], e // EW + 1)
                    for j in range(HC):
                        if not (isinstance(g, int) and g == e == 0):
                            pe.wait_ge(m["gel_ready"], HC * (E * g + e - 1) + j + 1)
                        w = slice(j * P, (j + 1) * P)
                        pe.matmul(ps_u[j][:, :], w1lo[:, e, w], group_cols(h2hi, g), start=True, stop=False)
                        pe.matmul(ps_u[j][:, :], w1hi[:, e, w], group_cols(h2lo, g), start=False, stop=False)
                        pe.matmul(ps_u[j][:, :], w1hi[:, e, w], group_cols(h2hi, g), start=False, stop=True).then_inc(m["u_ready"], 1)

                def spread(g, e):
                    i = E * g + e
                    pe.wait_ge(m["gT_ready"], g + 1)
                    pe.wait_ge(m["gbc_ready"], i)
                    pe.matmul(ps_gb[:, :], sel[:, e, :], gT, start=True, stop=True).then_inc(m["gb_ps"], 1)

                def down(g, e):
                    i = E * g + e
                    if not (isinstance(g, int) and g == e == 0):
                        pe.wait_ge(m["gated"], ONE + i - 1)
                    mm = None
                    for j in range(HC):
                        if j % HB == 0:
                            pe.wait_ge(m["sp_ready"], 2 * i + j // HB + 1)
                        w, at = slice(j * P, (j + 1) * P), e % 2
                        pe.matmul(ps_o[at][:, :], w2lo[:, e, w], sphi[:, at, j, :], start=(j == 0), stop=False)
                        pe.matmul(ps_o[at][:, :], w2hi[:, e, w], splo[:, at, j, :], start=False, stop=False)
                        mm = pe.matmul(ps_o[at][:, :], w2hi[:, e, w], sphi[:, at, j, :], start=False, stop=(j == HC - 1))
                    mm.then_inc(m["o_ready"], 1)

                def turn_gates(g):
                    pe.wait_ge(m["gcur_ready"], g + 1)
                    if not (isinstance(g, int) and g == 0):
                        pe.wait_ge(m["y_done"], ONE + g - 1)
                    for t in range(TG):
                        mm = pe.transpose(ps_x[0:WROWS, t * P:(t + 1) * P], gcur[:, t * WROWS:(t + 1) * WROWS], ident[:, :])
                    mm.then_inc(m["gT_ps"], 1)

                def turn_out(g, last):
                    pe.wait_ge(m["outT_done"], g + 1)
                    if not last:
                        pe.wait_ge(m["gT_ready"], g + 2)
                    for t in range(TG):
                        mm = pe.transpose(ps_x[:, t * P:(t + 1) * P], outT[:, t * P:(t + 1) * P], ident[:, :])
                    mm.then_inc(m["fin_ps"], 1)

                up(0, 0)
                slot(NG + 1)
                pe.wait_ge(s["w_split"], 2 * WCH)
                pe.wait_ge(s["sel_ready"], 2)
                pe.wait_ge(s["x2_done"], NG)
                pe.wait_ge(s["lg_ready"], ONE + NG)
                turn_gates(0)
                up(0, 1)
                spread(0, 0)
                down(0, 0)
                with pe.Fori(0, NG - 1) as g:
                    for e in range(1, E):
                        spread(g, e)
                        if e < E - 1:
                            up(g, e + 1)
                        else:
                            up(g + 1, 0)
                            turn_gates(g + 1)
                        down(g, e)
                    up(g + 1, 1)
                    turn_out(g, False)
                    spread(g + 1, 0)
                    down(g + 1, 0)
                for e in range(1, E):
                    spread(NG - 1, e)
                    if e < E - 1:
                        up(NG - 1, e + 1)
                    down(NG - 1, e)
                turn_out(NG - 1, True)

            @block.scalar
            def _(act):
                act.dma_start(xk[:, :], xk_dram).then_inc(xk_in, 16)
                act.dma_start(wm_sb, wmod).then_inc(wm_in, 16)
                act.dma_start(k_sb[:, :, :], k_dram).then_inc(k_in, 16)
                act.dma_start(v_sb[:, :, :], v_dram).then_inc(v_in, 16)
                act.dma_start(wr_sb[:, :], Wr).then_inc(router_in, 16)
                act.dma_start(br_sb[:, :], br.rearrange("(a e) -> a e", a=1).broadcast_to([P, E])).then_inc(router_in, 16)
                act.wait_ge(s["cols_ready"], 1)
                act.activation(sil[:, 0, :], cc, ACT.Exp, scale=-1.0).then_inc(s["cexp"], 1)

                def input_T(n):
                    wait_all(act, s["modg_ready"], 1, (s["ht_ps"], n + 1), (s["scores_ready"], TG * n))
                    act.activation(ht[:, :], ps_h[:, :], ACT.Identity, bias=col_of(SA, n),
                                   scale=col_of(CA, n)).then_inc(s["ht_ready"], 1)

                def exps(n, t):
                    if t == 0 and not (isinstance(n, int) and n == 0):
                        act.wait_ge(s["rinv_ready"], n)
                    act.wait_ge(s["nmax_ready"], TG * n + t + 1)
                    act.activation(probs[:, t % 2, :], ps_s[t % 2][:, :], ACT.Exp, bias=nmax[:, t:t + 1],
                                   accum_out=rsum[:, t:t + 1]).then_inc(s["exp_done"], 1)

                def probs_T(n, t):
                    act.wait_ge(s["pt_ps"], TG * n + t + 1)
                    act.activation(pt[:, :, t * P:(t + 1) * P], ps_pt[t % 2][:, :].rearrange("p (c n) -> p c n", c=KC),
                                   ACT.Copy).then_inc(s["pt_ready"], 1)

                def sums_T(n):
                    wait_all(act, s["modg_ready"], 1, (s["pv_done"], n + 1),
                             *([] if isinstance(n, int) and n == 0 else [(s["back_ps"], n)]))
                    act.activation(att[:, :], ps_av[:, :], ACT.Copy, scale=col_of(GA, n)).then_inc(s["att_ready"], 1)

                def input2_T(n):
                    wait_all(act, s["modg_ready"], 1, (s["h2_ps"], ONE + n + 1), (s["log_ps"], ONE + n), (s["h2_split"], ONE + n))
                    act.activation(h2[:, :], ps_h[:, :], ACT.Identity, bias=col_of(SB, n), scale=col_of(CB, n))
                    act.activation(group_cols(h2hi, n), ps_h[:, :], ACT.Identity, bias=col_of(SB, n),
                                   scale=col_of(CB, n)).then_inc(s["h2_ready"], 1)

                def gate_exp(n):
                    act.wait_ge(s["dlt_ready"], n + 1)
                    act.wait_ge(s["em_ready"], ONE + n)
                    act.activation(ex[:, :, :], dlt[:, :, :], ACT.Exp).then_inc(s["ex_ready"], 1)

                def slot(n):
                    group, before, before2, after = (has(n, n + i) for i in (0, -1, -2, 1))
                    if group:
                        exps(n, 0)
                        exps(n, 1)
                    if before:
                        sums_T(n - 1)
                    if group:
                        probs_T(n, 0)
                    if before2:
                        input2_T(n - 2)
                    if group:
                        exps(n, 2)
                        probs_T(n, 1)
                        exps(n, 3)
                        probs_T(n, 2)
                    if after:
                        input_T(n + 1)
                    if group:
                        probs_T(n, 3)
                    if isinstance(n, int):
                        for i in W_SLOT.get(n, ()):
                            act.wait_ge(w_in[i], 16 if i < WCH else 16 * EW)
                            act.activation(whi[i], wraw[:, i % 2, :].rearrange("p (e h) -> p e h", e=EW),
                                           ACT.Copy).then_inc(s["w_hi"], 1)
                    if before2:
                        gate_exp(n - 2)

                input_T(0)
                for b in range(B):
                    act.wait_ge(s["ks_ps"], b + 1)
                    act.activation(group_cols(kT, b), ps_k[b][:, :], ACT.Copy).then_inc(s["kT_ready"], 1)
                slots(act, slot)
                slot(NG + 1)

                HB = HC // 2

                def gelus(g, e):
                    i = E * g + e
                    for j in range(HC):
                        act.wait_ge(m["u_ready"], HC * i + j + 1)
                        if j % HB == 0 and not (isinstance(g, int) and g == 0 and e < 2):
                            act.wait_ge(m["sp_ready"], 2 * (i - 2) + j // HB + 1)
                        n = e * HC + j
                        act.activation(gel[:, e % 2, j, :], ps_u[j][:, :], ACT.Gelu,
                                       bias=b1c[:, n:n + 1]).then_inc(m["gel_ready"], 1)

                def gate_out(g, e):
                    i = E * g + e
                    act.wait_ge(m["gb_ps"], i + 1)
                    if not (isinstance(g, int) and g == e == 0):
                        act.wait_ge(m["gated"], ONE + i - 1)
                    act.activation(gbc[:, e % 2, :], ps_gb[:, :], ACT.Copy).then_inc(m["gbc_ready"], 1)

                def gates_T(g):
                    act.wait_ge(m["gT_ps"], g + 1)
                    act.wait_ge(m["gb_ps"], E * g)
                    act.activation(gT, ps_x[0:WROWS, :], ACT.Copy).then_inc(m["gT_ready"], 1)

                def scale_out(g):
                    wait_all(act, s["back_ps"], NG, (m["added"], ONE + (E - 1) * (g + 1)), (m["fin_ps"], ONE + g))
                    act.activation(outT[:, :], acc, ACT.Copy, scale=col_of(GBM, g)).then_inc(m["outT_done"], 1)

                gates_T(0)
                gelus(0, 0)
                gelus(0, 1)
                gate_out(0, 0)
                with act.Fori(0, NG - 1) as g:
                    for e in range(1, E):
                        gate_out(g, e)
                        if e < E - 1:
                            gelus(g, e + 1)
                        else:
                            gelus(g + 1, 0)
                            gates_T(g + 1)
                    scale_out(g)
                    gelus(g + 1, 1)
                    gate_out(g + 1, 0)
                for e in range(1, E):
                    gate_out(NG - 1, e)
                    if e < E - 1:
                        gelus(NG - 1, e + 1)
                scale_out(NG - 1)

            @block.vector
            def _(dve):
                for name in ("lg_ready", "em_ready"):
                    dve.sem_inc(s[name], ONE)
                dve.sem_inc(m["gated"], ONE)
                dve.sem_inc(m["y_done"], ONE)
                dve.wait_ge(s["rows_T"], 1)
                dve.tensor_copy(cols[:, :], ps_s[0][:, 0:R]).then_inc(s["cols_ready"], 1)
                dve.wait_ge(xk_in, 16)
                dve.bn_stats(kst[:, :], xk[:, :]).then_inc(s["k_stat"], 1)
                dve.wait_ge(s["k_stat"], 1)
                dve.bn_aggr(kmv[:, 0:2], kst[:, :]).then_inc(s["k_aggr"], 1)
                dve.wait_ge(s["k_aggr"], 1)
                dve.tensor_scalar(kmv[:, 2:3], kmv[:, 1:2], EPS, None, ALU.add).then_inc(s["k_var"], 1)
                dve.wait_ge(s["cexp"], 1)
                dve.tensor_scalar(sil[:, 1, :], sil[:, 0, :], 1.0, None, ALU.add).then_inc(s["c1"], 1)
                dve.wait_ge(s["c1"], 1)
                dve.reciprocal(sil[:, 0, :], sil[:, 1, :]).then_inc(s["crec"], 1)
                dve.wait_ge(s["crec"], 1)
                dve.wait_ge(s["cols_ready"], 1)
                dve.tensor_tensor(sil[:, 2, :], cc, sil[:, 0, :], ALU.mult).then_inc(s["sil_ready"], 1)
                dve.wait_ge(s["k_rstd"], 1)
                dve.tensor_scalar(xkh[:, :], xk[:, :], kmv[:, 0:1], kmv[:, 3:4], ALU.subtract, ALU.mult).then_inc(s["xkh_ready"], 1)

                def modulation():
                    dve.wait_ge(s["mod_ps"], 1)
                    dve.tensor_copy(mod[:, :, :], ps_log[:, 0:MODS * B].rearrange("p (m b) -> p m b", b=B)).then_inc(s["mod_copied"], 1)
                    dve.wait_ge(s["mod_copied"], 1)
                    dve.tensor_scalar(mod[:, CA, :], mod[:, CA, :], 1.0, None, ALU.add)
                    dve.tensor_scalar(mod[:, CB, :], mod[:, CB, :], 1.0, None, ALU.add)
                    for n, mo in enumerate((GA, GBM)):
                        dve.tensor_scalar(gsgn[:, n, 0, :], mod[:, mo, :], 0.0, 2.0, ALU.is_ge, ALU.mult).then_inc(s["mod_step"], 1)
                        dve.scalar_tensor_tensor(out=gsgn[:, n, 1, :], in0=mod[:, mo, :], scalar=-1.0, in1=mod[:, mo, :],
                                                 op0=ALU.mult, op1=ALU.max).then_inc(s["mod_step"], 1)
                    dve.wait_ge(s["mod_step"], 4)
                    dve.tensor_scalar(gsgn[:, :, 0, :], gsgn[:, :, 0, :], -1.0, None, ALU.add).then_inc(s["mod_step"], 1)
                    dve.tensor_scalar(gsgn[:, :, 1, :], gsgn[:, :, 1, :], 0.25, None, ALU.max).then_inc(s["mod_step"], 1)
                    dve.wait_ge(s["mod_step"], 6)
                    for n, mo in enumerate((GA, GBM)):
                        dve.tensor_tensor(mod[:, mo, :], gsgn[:, n, 0, :], gsgn[:, n, 1, :], ALU.mult).then_inc(s["mod_ready"], 1)
                    dve.wait_ge(s["mod_ready"], 2)
                    for g in range(GB):
                        op = dve.tensor_copy(mod_g[:, :, :].rearrange("p m (b g) -> p m b g", g=GB)[:, :, :, g], mod[:, :, :])
                    op.then_inc(s["modg_ready"], 1)

                def scale_keys():
                    dve.wait_ge(s["kfac_ps"], 1)
                    for b in range(B):
                        dve.tensor_scalar(kfac[:, b, :], ps_s[1][:, b * KC:(b + 1) * KC], mod[:, CA, b:b + 1],
                                          mod[:, SA, b:b + 1], ALU.mult, ALU.add).then_inc(s["kfac_ready"], 1)
                    dve.wait_ge(k_in, 16)
                    dve.wait_ge(s["kfac_ready"], B)
                    for b in range(B):
                        for j in range(KC):
                            op = dve.tensor_scalar(ks[:, b, j, :], k_sb[:, j, :], kfac[:, b, j:j + 1], None, ALU.mult)
                        op.then_inc(s["ks_ready"], 1)

                def tile_of(n, t):
                    if isinstance(n, int):
                        return x_sb[:, TG * n + t, :]
                    return x_sb[:, bass.ds(TG * n + t, 1), :].rearrange("p a d -> p (a d)")

                def stats(which, n):
                    i = which - 1
                    first = isinstance(n, int) and n == 0
                    before = [] if first else [(s[f"aggr{which}"], TG * n)]
                    if which == 2:
                        before.append((s["x2_done"], n + 1))
                    wait_all(dve, x_in[0], 16, *before)
                    for t in range(TG):
                        dve.bn_stats(st[:, i, t, :], tile_of(n, t)).then_inc(s[f"stat{which}"], 1)
                    wait_all(dve, x_in[0], 16, (s[f"stat{which}"], TG * n + TG),
                             *([] if first else [(s[f"xhat{which}"], n)]))
                    for t in range(TG):
                        dve.bn_aggr(mv[:, i, t, :], st[:, i, t, :]).then_inc(s[f"aggr{which}"], 1)
                    dve.wait_ge(s[f"aggr{which}"], TG * n + TG)
                    dve.tensor_scalar(veps[:, i, :], mv[:, i, :, 1], EPS, None, ALU.add).then_inc(s[f"var{which}"], 1)

                def normalize(which, n):
                    i = which - 1
                    dve.wait_ge(s[f"rstd{which}"], n + 1)
                    if which == 2:
                        dve.wait_ge(s["h2_ps"], ONE + n)
                    elif not (isinstance(n, int) and n == 0):
                        dve.wait_ge(s["ht_ps"], n)
                    for t in range(TG):
                        op = dve.tensor_scalar(xh[:, i, t, :], tile_of(n, t), mv[:, i, t, 0:1], rstd[:, i, t:t + 1],
                                               ALU.subtract, ALU.mult)
                    op.then_inc(s[f"xhat{which}"], 1)

                def maxima(n, t):
                    dve.wait_ge(s["scores_ready"], TG * n + t + 1)
                    dve.tensor_reduce(nmax[:, t:t + 1], ps_s[t % 2][:, :], AX_X, ALU.max,
                                      negate=True).then_inc(s["nmax_ready"], 1)

                def denominators(n):
                    dve.wait_ge(s["exp_done"], TG * (n + 1))
                    if not (isinstance(n, int) and n == 0):
                        dve.wait_ge(s["x2_done"], n)
                    dve.reciprocal(rinv[:, :], rsum[:, :]).then_inc(s["rinv_ready"], 1)

                def residual(n):
                    dve.wait_ge(s["back_ps"], n + 1)
                    dve.wait_ge(s["rinv_ready"], n + 1)
                    for t in range(TG):
                        xt = tile_of(n, t)
                        op = dve.scalar_tensor_tensor(out=xt, in0=ps_back[:, t * P:(t + 1) * P], scalar=rinv[:, t:t + 1],
                                                      in1=xt, op0=ALU.mult, op1=ALU.add)
                    op.then_inc(s["x2_done"], 1)

                def gate_logits(n):
                    dve.wait_ge(s["log_ps"], ONE + n + 1)
                    dve.wait_ge(router_in, 32)
                    dve.tensor_tensor(lg[:, :, :], ps_log[:, 0:TG * E].rearrange("p (t e) -> p t e", e=E),
                                      br_sb[:, :].unsqueeze(1).to_broadcast([P, TG, E]), ALU.add).then_inc(s["lg_ready"], 1)
                    wait_all(dve, router_in, 32, (s["lg_ready"], ONE + n + 1))
                    for t in range(TG):
                        op = dve.max(top[:, t, :], lg[:, t, :])
                    op.then_inc(s["top_ready"], 1)
                    dve.wait_ge(s["top_ready"], n + 1)
                    dve.tensor_tensor(dlt[:, :, :], lg[:, :, :], top[:, :, 0:1].to_broadcast([P, TG, E]),
                                      ALU.subtract).then_inc(s["dlt_ready"], 1)
                    dve.tensor_tensor(keep[:, :, :], lg[:, :, :], top[:, :, 1:2].to_broadcast([P, TG, E]),
                                      ALU.is_ge).then_inc(s["keep_ready"], 1)

                def gate_weights(n):
                    dve.wait_ge(s["ex_ready"], n + 1)
                    dve.wait_ge(s["keep_ready"], n + 1)
                    dve.tensor_tensor(em[:, :, :], ex[:, :, :], keep[:, :, :], ALU.mult).then_inc(s["em_ready"], 1)
                    dve.wait_ge(s["em_ready"], ONE + n + 1)
                    dve.tensor_reduce(esum[:, :], em[:, :, :], AX_X, ALU.add).then_inc(s["esum_ready"], 1)
                    dve.wait_ge(s["esum_ready"], n + 1)
                    dve.reciprocal(einv[:, :], esum[:, :]).then_inc(s["einv_ready"], 1)
                    dve.wait_ge(s["einv_ready"], n + 1)
                    dve.tensor_tensor(wgt[:, :, :], em[:, :, :], einv[:, :].unsqueeze(2).to_broadcast([P, TG, E]),
                                      ALU.mult).then_inc(s["wgt_ready"], 1)
                    dve.wait_ge(s["wgt_ready"], n + 1)
                    gt = row_of(gates, n).rearrange("p (t w) -> p t w", w=WROWS)
                    dve.tensor_copy(gt[:, :, 0:E].bitcast(F32R), wgt[:, :, :]).then_inc(s["gate_hi"], 1)
                    dve.wait_ge(s["gate_hi"], n + 1)
                    dve.tensor_tensor(gt[:, :, E:WROWS].bitcast(F32R), wgt[:, :, :], gt[:, :, 0:E],
                                      ALU.subtract).then_inc(s["gates_ready"], 1)

                def slot(n):
                    group, before, before2, after = (has(n, n + i) for i in (0, -1, -2, 1))
                    if before:
                        denominators(n - 1)
                    if group:
                        maxima(n, 0)
                        maxima(n, 1)
                    if before2:
                        normalize(2, n - 2)
                    if after:
                        if isinstance(n, int) and n == 0:
                            for i in range(1, B):
                                dve.wait_ge(x_in[i], 16)
                        stats(1, n + 1)
                        normalize(1, n + 1)
                    if group:
                        maxima(n, 2)
                        maxima(n, 3)
                    if before2:
                        gate_logits(n - 2)
                    if before:
                        residual(n - 1)
                        stats(2, n - 1)
                    if before2:
                        gate_weights(n - 2)

                dve.wait_ge(x_in[0], 16)
                stats(1, 0)
                normalize(1, 0)
                modulation()
                scale_keys()
                slots(dve, slot)
                slot(NG + 1)

                HB = HC // 2
                dve.wait_ge(s["w_split"], 2 * WCH)

                def split(g, e):
                    i = E * g + e
                    for half in range(2):
                        c = slice(half * HB, (half + 1) * HB)
                        dve.wait_ge(m["gel_ready"], HC * i + (half + 1) * HB)
                        dve.tensor_copy(sphi[:, e % 2, c, :], gel[:, e % 2, c, :]).then_inc(m["sp_hi"], 1)
                        dve.wait_ge(m["sp_hi"], 2 * i + half + 1)
                        dve.tensor_tensor(splo[:, e % 2, c, :], gel[:, e % 2, c, :], sphi[:, e % 2, c, :].bitcast(F32),
                                          ALU.subtract).then_inc(m["sp_ready"], 1)

                def gate(g, e):
                    i = E * g + e
                    dve.wait_ge(m["o_ready"], i + 1)
                    dve.wait_ge(m["gbc_ready"], i + 1)
                    if e == 0:
                        dve.wait_ge(m["outT_done"], g)
                    else:
                        dve.wait_ge(m["added"], ONE + (E - 1) * g + max(e - 2, 0))
                    dve.scalar_tensor_tensor(out=acc if e == 0 else msk[:, e % 2, :], in0=ps_o[e % 2][:, :],
                                             scalar=b2c[:, e:e + 1], in1=gbc[:, e % 2, :],
                                             op0=ALU.add, op1=ALU.mult).then_inc(m["gated"], 1)

                def finish(g):
                    dve.wait_ge(m["fin_ps"], ONE + g + 1)
                    at = group_tiles(g)
                    dve.tensor_tensor(x_sb[:, at, :], ps_x[:, :].rearrange("p (t d) -> p t d", d=D), x_sb[:, at, :],
                                      ALU.add).then_inc(m["y_done"], 1)

                split(0, 0)
                split(0, 1)
                gate(0, 0)
                with dve.Fori(0, NG - 1) as g:
                    for e in range(1, E):
                        if e < E - 1:
                            split(g, e + 1)
                        else:
                            split(g + 1, 0)
                        gate(g, e)
                    split(g + 1, 1)
                    finish(g)
                    gate(g + 1, 0)
                for e in range(1, E):
                    if e < E - 1:
                        split(NG - 1, e + 1)
                    gate(NG - 1, e)
                finish(NG - 1)


_INS = ['L0_attn_q', 'L0_attn_k', 'L0_attn_v', 'L0_ffn_W1', 'L0_ffn_b1', 'L0_ffn_W2', 'L0_ffn_b2',
        'L0_ffn_Wr', 'L0_ffn_br', 'L0_c', 'L0_wmod']


def kernel(**inputs):
    import numpy as _np
    import concourse.bacc as _bacc
    from concourse import mybir as _mybir
    from concourse.bass_utils import run_bass_kernel_spmd as _run

    nc = _bacc.Bacc("TRN2", target_bir_lowering=False, num_devices=1)
    arrays, args = {}, []
    for name in _INS:
        a = _np.ascontiguousarray(inputs[name])
        arrays[f"in_{name}_dram"] = a
        args.append(nc.dram_tensor(f"in_{name}_dram", a.shape, _mybir.dt.from_np(a.dtype), kind="ExternalInput").ap())
    out = nc.dram_tensor("out_0_dram", inputs['L0_attn_q'].shape, _mybir.dt.float32, kind="ExternalOutput").ap()
    adaln_block(nc, *args, out)
    r = _run(nc, [arrays], core_ids=[0])
    return r.results[0]["out_0_dram"]
```

```python
from contextlib import ExitStack

import concourse.bass as bass
from concourse import mybir

ALU = mybir.AluOpType
ACT = mybir.ActivationFunctionType
F32 = mybir.dt.float32
F32R = mybir.dt.float32r
AX_X = mybir.AxisListType.X

P = 128
TG = 4
GT = TG * P
SPLIT = 2


def adaln_block(nc, q, k, v, W1, b1, W2, b2, Wr, br, c, wmod, out):
    B, S, D = q.shape
    T = k.shape[1]
    E, _, H = W1.shape
    MODS = wmod.shape[1] // D
    KC = T // P
    HC = H // P
    NT = B * S // P
    NG = NT // TG
    GB = NG // B
    STEP = S // 4
    EPS = 1e-5
    R = E * HC + E
    HB = HC // 2
    EW = 2
    NW = 2 * (E // EW)
    GS = 4
    SA, CA, SB, CB, GBM = range(5)
    PART = {SA: 0, CA: 1, SB: 3, CB: 4, GBM: 5}
    GA_PART = 2
    WM_A = 2 * P
    assert D == P and T == GT and GB == 2 and MODS == 6 and KC == 4 and H == GT and E == 8

    with ExitStack() as ctx:
        def sb(name, shape, dt=F32):
            return ctx.enter_context(nc.sbuf_tensor(name, shape, dt))

        def sem(name):
            return ctx.enter_context(nc.semaphore(name))

        x_sb = sb("x_sb", [P, NT, D])
        w1hi = sb("w1hi", [P, E, H], F32R)
        w1lo = sb("w1lo", [P, E, H], F32R)
        w2hi = sb("w2hi", [P, E, HC * D], F32R)
        w2lo = sb("w2lo", [P, E, HC * D], F32R)
        h2hi = sb("h2hi", [P, 2 * GT], F32R)
        h2lo = sb("h2lo", [P, 2 * GT], F32R)
        wraw = sb("wraw", [P, 2, EW, H])
        gel = sb("gel", [P, 2, HC, GT])
        sphi = sb("sphi", [P, 2, HC, GT], F32R)
        splo = sb("splo", [P, 2, HC, GT], F32R)
        wm_sb = gel[:, 0, 0:2, :].rearrange("p a b -> p (a b)")[:, 0:MODS * D]
        ks = gel[:, 1, :, :].rearrange("p b (n d) -> p b n d", d=D)
        kT = sb("kT", [P, B * T])
        k_sb = sb("k_sb", [P, KC, D])
        v_sb = sb("v_sb", [P, KC * D])
        vg = sb("vg", [P, B * KC * D])
        pt = sb("pt", [P, KC, GT])
        probs = sb("probs", [P, 2, T])
        xh = sb("xh", [P, 2, TG, D])
        ht = sb("ht", [P, GT])
        h2 = sb("h2", [P, GT])
        acc = sb("acc", [P, GT])
        msk = sb("msk", [P, 2, GT])
        outT = sb("outT", [P, GT])
        gbc = sb("gbc", [P, GS, GT])
        gT = sb("gT", [E, GT])
        ident = sb("ident", [P, P])
        rows = outT[0:R, 0:P]
        c_sb = sb("c_sb", [B, D])
        cc = sb("cc", [P, B])
        ga_raw, ga_abs, ga_sign = acc, msk[:, 0, :], msk[:, 1, :]
        cols = sb("cols", [P, R])
        sil = sb("sil", [P, 3, B])
        mod = sb("mod", [P, MODS - 1, B])
        gsgn = sb("gsgn", [P, 2, B])
        mod_g = sb("mod_g", [P, MODS - 1, NG])
        xk = sb("xk", [B * KC, D])
        xkh = sb("xkh", [B * KC, D])
        kst = sb("kst", [B * KC, 6])
        kmv = sb("kmv", [B * KC, 4])
        kfac = sb("kfac", [P, B, KC])
        wr_sb = sb("wr_sb", [P, E])
        br_sb = sb("br_sb", [P, E])
        st = sb("st", [P, 2, TG, 6])
        mv = sb("mv", [P, 2, TG, 2])
        veps = sb("veps", [P, 2, TG])
        rstd = sb("rstd", [P, 2, TG])
        mhalf = sb("mhalf", [P, TG])
        warm = sb("warm", [P, 2])
        nmax = sb("nmax", [P, TG])
        rsum = sb("rsum", [P, TG])
        rinv = sb("rinv", [P, TG])
        lg = sb("lg", [P, TG, E])
        top = sb("top", [P, TG, 8])
        dlt = sb("dlt", [P, TG, E])
        keep = sb("keep", [P, TG, E])
        ex = sb("ex", [P, TG, E])
        em = sb("em", [P, TG, E])
        esum = sb("esum", [P, TG])
        einv = sb("einv", [P, TG])
        wgt = sb("wgt", [P, TG, E])
        b1c = cols[:, 0:E * HC]
        b2c = cols[:, E * HC:E * HC + E]

        ps = [ctx.enter_context(nc.psum_tensor(f"ps{i}", [P, GT], F32)) for i in range(8)]
        ps_u, ps_o, ps_s, ps_x = ps[0:4], ps[4], ps[5:7], ps[7]
        ps_k, ps_rows, ps_kfac, ps_mod, ps_ga = (ps[0], ps[1], ps[2], ps[1]), ps[5], ps[3], ps[6], ps[4]
        ps_c, ps_mod2 = ps[7], ps[2]

        def first(g):
            return isinstance(g, int) and g == 0

        def scores_bank(n, t):
            return (ps_s[0], ps_s[1], ps_o, ps_u[0])[t] if isinstance(n, int) and n < 2 else ps_s[t % 2]

        def sums_bank(n, t):
            return (ps_u[3], ps_s[0], ps_s[1], ps_o)[t] if first(n) else ps_x

        def turned_bank(n, t):
            return ps_u[1 + t % 2] if isinstance(n, int) and n == 1 else ps_x

        ONE = 1

        wm_in = [sem(f"wm_in{i}") for i in range(2)]
        c_in, rows_in, xk_in, k_in, v_in, router_in = map(sem, (
            "c_in", "rows_in", "xk_in", "k_in", "v_in", "router_in"))
        x_in = [sem(f"x_in{i}") for i in range(B)]
        x1_in = sem("x1_in")
        w_in = [sem(f"w_in{i}") for i in range(NW)]
        names = """zeroed ident_ready c_T cc_ready rows_T cols_ready cexp c1 crec sil_ready mod_ps mod_copied
            mod_ready mod_step modg_ready k_stat k_aggr k_var k_rstd xkh_ready kfac_ps kfac_ready ks_ready
            ks_ps kT_ready ga_ps ga_copied ga_step vg_ready w_hi w1_split w2_split""".split()
        names += """stat1 aggr1 var1 rstd1 xhat1 ht_ps ht_ready scores_ready nmax_ready exp_done pt_ps pt_ready
            pv_done x2_tile x2_done rinv_ready stat2 aggr2 var2 rstd2 xhat2 h2_ps h2_ready h2_hi h2_split
            log_ps lg_ready top_ready dlt_ready keep_ready ex_ready em_ready esum_ready einv_ready
            wgt_ready gT_ps gT_ready""".split()
        s = {n: sem(n) for n in names}
        names = "u_ready gel_ready sp_hi sp_ready o_ready gated added outT_done fin_ps y_done out_done".split()
        m = {n: sem("moe_" + n) for n in names}
        gbc_in = [sem(f"gbc_in{i}") for i in range(GS)]

        x_dram = q.rearrange("b s d -> (b s) d").rearrange("(n p) d -> p n d", p=P)
        xk_dram = q.rearrange("b (j r) d -> (b j) r d", r=STEP)[:, 0, :]
        out_dram = out.rearrange("b s d -> (b s) d").rearrange("(n p) d -> p n d", p=P)
        k_dram = k[0].rearrange("(n p) d -> p n d", p=P)
        v_dram = v[0].rearrange("(n p) d -> p n d", p=P)
        w1_dram = W1.rearrange("e d h -> d e h")
        w2_dram = W2.rearrange("e (c p) d -> p e c d", p=P)

        def piece(w1, w2, i):
            return (w1, w2)[i % 2][:, EW * (i // 2):EW * (i // 2 + 1), :]

        raw = [wraw[:, 0, :, :], wraw[:, 1, :, :], gbc[:, 0:EW, :], gbc[:, EW:GS, :], msk[:, :, :],
               wraw[:, 0, :, :], wraw[:, 1, :, :], wraw[:, 0, :, :]]
        RAW_WAIT = {4: (s["ga_step"], 4),
                    5: (s["w1_split"], 1), 6: (s["w2_split"], 1), 7: (s["w2_split"], 3)}

        def wait_all(eng, loaded, value, *counted):
            counted = [(of, n if isinstance(n, int) else eng.to_reg(n)) for of, n in counted]
            eng.wait_ge(loaded, value)
            for of, n in counted:
                eng.wait_ge(of, n)

        def slot_cols(t, g):
            if isinstance(g, int):
                return t[:, (g % 2) * GT:(g % 2 + 1) * GT]
            return t[:, bass.ts(g % 2, GT)]

        def batch_cols(t, g, width):
            b = g // GB if isinstance(g, int) else g >> (GB - 1)
            return t[:, b * width:(b + 1) * width] if isinstance(g, int) else t[:, bass.ts(b, width)]

        def group_tiles(g):
            return slice(g * TG, (g + 1) * TG) if isinstance(g, int) else bass.ts(g, TG)

        def col_of(mo, g):
            return mod_g[:, mo, g:g + 1] if isinstance(g, int) else mod_g[:, mo, bass.ds(g, 1)]

        def rounds(eng, do):
            do(0, before=False, att=True, inp=True, soft=False)
            with eng.Fori(1, NG - 2) as g:
                do(g, before=True, att=True, inp=True)
            do(NG - 2, before=True, att=True, inp=False)
            do(NG - 1, before=True, att=False, inp=False)

        with nc.Block() as block:

            @block.sync
            def _(sp):
                sp.dma_start(c_sb[:, :], c).then_inc(c_in, 16)
                sp.dma_start(wm_sb[:, 0:WM_A], wmod[:, 0:WM_A]).then_inc(wm_in[0], 16)

                def load_x(i):
                    t = slice(NT // B * i, NT // B * (i + 1))
                    sp.dma_start(x_sb[:, t, :], x_dram[:, t, :]).then_inc(x_in[i], 16)

                def load_x0(g):
                    sp.dma_start(x_sb[:, group_tiles(g), :], x_dram[:, group_tiles(g), :]).then_inc((x_in[0], x1_in)[g], 16)

                def load_w(i):
                    if i in RAW_WAIT:
                        sp.wait_ge(*RAW_WAIT[i])
                    e0 = EW * (i // 2)
                    dst = raw[i]
                    if i % 2 == 0:
                        sp.dma_start(dst, w1_dram[:, e0:e0 + EW, :]).then_inc(w_in[i], 16)
                    else:
                        for j in range(EW):
                            sp.dma_start(dst[:, j, :].rearrange("p (c d) -> p c d", c=HC),
                                         w2_dram[:, e0 + j, :, :]).then_inc(w_in[i], 16)

                load_x0(0)
                sp.dma_start(rows[0:E * HC, :], b1.rearrange("e (c p) -> (e c) p", p=P)).then_inc(rows_in, 16)
                sp.dma_start(rows[E * HC:E * HC + E, :], b2).then_inc(rows_in, 16)
                load_x0(1)
                for i in range(4):
                    load_w(i)
                load_x(1)
                for i in range(4, NW - 1):
                    load_w(i)
                for i in range(2, B):
                    load_x(i)

                def broadcast(g, e):
                    if e == 0:
                        sp.wait_ge(s["gT_ready"], g + 1)
                    if first(g) and e < GS:
                        sp.wait_ge(s["w1_split" if e < EW else "w2_split"], 2)
                    else:
                        sp.wait_ge(m["gated"], E * g + e - GS + 1)
                    sp.dma_start(gbc[:, e % GS, :], gT[e:e + 1, :].unsqueeze(1).to_broadcast([1, P, GT])).then_inc(gbc_in[e % GS], 16)

                def store(g):
                    sp.wait_ge(m["y_done"], g + 1)
                    sp.dma_start(out_dram[:, group_tiles(g), :], x_sb[:, group_tiles(g), :]).then_inc(m["out_done"], 16)

                def round_(g, before, att, inp, soft=True):
                    soft = soft and att
                    for e in range(E):
                        broadcast(g, e)
                        if first(g) and e == GS - 1:
                            load_w(NW - 1)
                    if before:
                        store(g - 1)

                rounds(sp, round_)
                store(NG - 1)
                sp.wait_ge(m["out_done"], 16 * NG)

            @block.gpsimd
            def _(pool):
                pool.memset(mhalf[:, :], -0.5).then_inc(s["zeroed"], 1)
                pool.memset(ident[:, :], 0.0).then_inc(s["zeroed"], 1)
                pool.wait_ge(s["zeroed"], 2)
                pool.affine_select(out=ident[:, :], in_=ident[:, :], compare_op=ALU.not_equal, fill=1.0,
                                   base=0, pattern=[[-1, P]], channel_multiplier=1).then_inc(s["ident_ready"], 1)
                pool.wait_ge(s["k_var"], 1)
                pool.tensor_tensor(kmv[:, 3:4], kmv[:, 2:3], mhalf[0:B * KC, 0:1], ALU.pow).then_inc(s["k_rstd"], 1)

                def root(which, n):
                    pool.wait_ge(s[f"var{which}"], n + 1)
                    pool.tensor_tensor(rstd[:, which - 1, :], veps[:, which - 1, :], mhalf[:, :],
                                       ALU.pow).then_inc(s[f"rstd{which}"], 1)

                def split_w1(i):
                    pool.wait_ge(s["w_hi"], 2 * i + 1)
                    pool.tensor_tensor(piece(w1lo, w2lo, 2 * i), raw[2 * i], piece(w1hi, w2hi, 2 * i).bitcast(F32),
                                       ALU.subtract).then_inc(s["w1_split"], 1)

                def split_input(n):
                    pool.wait_ge(s["h2_hi"], n + 1)
                    pool.tensor_tensor(slot_cols(h2lo, n), h2[:, :], slot_cols(h2hi, n).bitcast(F32),
                                       ALU.subtract).then_inc(s["h2_split"], 1)

                def add(g, e):
                    pool.wait_ge(m["gated"], E * g + e + 1)
                    if e > 1:
                        pool.wait_ge(m["added"], (E - 1) * g + e - 1)
                    pool.tensor_tensor(acc[:, :], acc[:, :], msk[:, e % 2, :], ALU.add).then_inc(m["added"], 1)

                def scale_out(g):
                    wait_all(pool, s["modg_ready"], 1, (m["added"], (E - 1) * (g + 1)), (m["fin_ps"], ONE + g))
                    pool.tensor_tensor(outT[:, :], acc[:, :], col_of(GBM, g).to_broadcast([P, GT]), ALU.mult).then_inc(m["outT_done"], 1)

                root(1, 0)
                pool.wait_ge(v_in, 16)
                pool.wait_ge(s["ga_step"], 4)
                for b in range(B):
                    pool.tensor_tensor(vg[:, b * KC * D:(b + 1) * KC * D].rearrange("p (n d) -> p n d", d=D),
                                       v_sb[:, :].rearrange("p (n d) -> p n d", d=D),
                                       ga_raw[:, b * D:(b + 1) * D].unsqueeze(1).to_broadcast([P, KC, D]),
                                       ALU.mult).then_inc(s["vg_ready"], 1)
                root(1, 1)
                split_w1(0)
                root(2, 0)
                split_input(0)
                for i in range(1, NW // 2):
                    split_w1(i)

                def round_(g, before, att, inp, soft=True):
                    soft = soft and att
                    for e in range(E):
                        if e == 2 and inp:
                            root(1, g + 2)
                        if e == 3 and att:
                            root(2, g + 1)
                        if e == 5 and att:
                            split_input(g + 1)
                        if e > 0 and (att or e < E - 1):
                            add(g, e)
                    if att:
                        scale_out(g)

                rounds(pool, round_)

            @block.tensor
            def _(pe):
                pe.sem_inc(m["fin_ps"], ONE)
                pe.wait_ge(s["ident_ready"], 1)
                pe.wait_ge(c_in, 16)
                pe.transpose(ps_c[:, 0:B], c_sb[:, :], ident[0:B, 0:B]).then_inc(s["c_T"], 1)
                pe.wait_ge(s["sil_ready"], 1)
                pe.wait_ge(wm_in[0], 16)
                def modulate(to, mos):
                    for mo in mos:
                        part = PART[mo]
                        mm = pe.matmul(to[:, mo * B:(mo + 1) * B], wm_sb[:, part * D:(part + 1) * D], sil[:, 2, :],
                                       start=True, stop=True)
                    mm.then_inc(s["mod_ps"], 1)

                modulate(ps_mod, (SA, CA))
                pe.wait_ge(s["xkh_ready"], 1)
                pe.transpose(ps_kfac[:, 0:B * KC], xkh[:, :], ident[0:B * KC, 0:B * KC]).then_inc(s["kfac_ps"], 1)
                pe.wait_ge(wm_in[1], 16)
                modulate(ps_mod2, (SB, CB, GBM))
                pe.wait_ge(rows_in, 32)
                pe.transpose(ps_rows[:, 0:R], rows, ident[0:R, 0:R]).then_inc(s["rows_T"], 1)
                for b in range(B):
                    mm = pe.matmul(ps_ga[:, b * D:(b + 1) * D], sil[:, 2, b:b + 1].to_broadcast([P, P]),
                                   wm_sb[:, GA_PART * D:(GA_PART + 1) * D], start=True, stop=True)
                mm.then_inc(s["ga_ps"], 1)

                def turn(to, of):
                    for t in range(TG):
                        mm = pe.transpose(to[:, t * P:(t + 1) * P], of[:, t, :], ident[:, :])
                    return mm

                def turn_keys(b):
                    pe.wait_ge(s["ks_ready"], b + 1)
                    if b == 2:
                        pe.wait_ge(s["mod_copied"], 1)
                    if b == 3:
                        pe.wait_ge(s["kT_ready"], 2)
                    turn(ps_k[b], ks[:, b, :, :]).then_inc(s["ks_ps"], 1)


                def turn_input(n):
                    pe.wait_ge(s["xhat1"], n + 1)
                    if isinstance(n, int) and n == 1:
                        pe.wait_ge(s["pt_ready"], TG)
                    elif isinstance(n, int) and n == 2:
                        pe.wait_ge(s["lg_ready"], n)
                    elif not first(n):
                        pe.wait_ge(m["y_done"], n - 2)
                    turn(ps_x, xh[:, 0, :, :]).then_inc(s["ht_ps"], 1)

                def scores(n, t):
                    if t == 0:
                        pe.wait_ge(s["ht_ready"], n + 1)
                    if t >= 2 and not (isinstance(n, int) and n < 2):
                        pe.wait_ge(s["exp_done"], TG * n + t - 1)
                    pe.matmul(scores_bank(n, t)[:, :], ht[:, t * P:(t + 1) * P], batch_cols(kT, n, T),
                              start=True, stop=True).then_inc(s["scores_ready"], 1)

                def turn_probs(n, t):
                    pe.wait_ge(s["exp_done"], TG * n + t + 1)
                    if isinstance(n, int) and n == 1:
                        pe.wait_ge(*(s["kT_ready"], B) if t < 2 else (s["pt_ready"], TG + t - 1))
                    elif t > 0:
                        pe.wait_ge(s["pt_ready"], TG * n + t)
                    elif not first(n):
                        pe.wait_ge(s["gT_ready"], n)
                    turn(turned_bank(n, t), probs[:, t % 2, :].rearrange("p (c n) -> p c n", c=KC)).then_inc(s["pt_ps"], 1)

                def sums(n, tiles=range(TG)):
                    pe.wait_ge(s["pt_ready"], TG * n + tiles[-1] + 1)
                    if isinstance(n, int) and n == 1:
                        pe.wait_ge(s["gT_ready"], 1)
                    for t in tiles:
                        for j in range(KC):
                            mm = pe.matmul(sums_bank(n, t)[:, t * P:(t + 1) * P], pt[:, j, t * P:(t + 1) * P],
                                           batch_cols(vg, n, KC * D)[:, j * D:(j + 1) * D], start=(j == 0), stop=(j == KC - 1))
                        mm.then_inc(s["pv_done"], 1)

                def turn_input2(n):
                    pe.wait_ge(s["xhat2"], n + 1)
                    if first(n):
                        pe.wait_ge(s["ht_ready"], 2)
                    turn(ps_x, xh[:, 1, :, :]).then_inc(s["h2_ps"], 1)

                def logits(n):
                    pe.wait_ge(s["h2_ready"], n + 1)
                    for t in range(TG):
                        mm = pe.matmul(ps_x[:, t * E:(t + 1) * E], h2[:, t * P:(t + 1) * P], wr_sb[:, :],
                                       start=True, stop=True)
                    mm.then_inc(s["log_ps"], 1)

                def turn_gates(n, inp):
                    pe.wait_ge(s["wgt_ready"], n + 1)
                    if not first(n):
                        pe.wait_ge(*(s["ht_ready"], n + 2) if inp else (m["y_done"], n - 1))
                    for t in range(TG):
                        mm = pe.transpose(ps_x[0:E, t * P:(t + 1) * P], wgt[:, t, :], ident[:, :])
                    mm.then_inc(s["gT_ps"], 1)

                def turn_out(g, free, count):
                    pe.wait_ge(m["outT_done"], g + 1)
                    pe.wait_ge(free, count)
                    for t in range(TG):
                        mm = pe.transpose(ps_x[:, t * P:(t + 1) * P], outT[:, t * P:(t + 1) * P], ident[:, :])
                    mm.then_inc(m["fin_ps"], 1)

                def up(g, e):
                    if first(g) and e % EW == 0:
                        pe.wait_ge(s["w1_split"], e // EW + 1)
                    if e == 0:
                        pe.wait_ge(s["h2_split"], g + 1)
                    for j in range(HC):
                        if first(g) and e == 0 and j == 1:
                            pe.wait_ge(s["pt_ready"], 2 * TG)
                        if not (first(g) and e == 0):
                            pe.wait_ge(m["gel_ready"], HC * (E * g + e - 1) + j + 1)
                        w = slice(j * P, (j + 1) * P)
                        pe.matmul(ps_u[j][:, :], w1lo[:, e, w], slot_cols(h2hi, g), start=True, stop=False)
                        pe.matmul(ps_u[j][:, :], w1hi[:, e, w], slot_cols(h2lo, g), start=False, stop=False)
                        pe.matmul(ps_u[j][:, :], w1hi[:, e, w], slot_cols(h2hi, g), start=False, stop=True).then_inc(m["u_ready"], 1)

                def down(g, e):
                    i = E * g + e
                    if first(g) and e % EW == 0:
                        pe.wait_ge(s["w2_split"], e // EW + 1)
                    if not (first(g) and e == 0):
                        pe.wait_ge(m["gated"], i)
                    for j in range(HC):
                        if j % HB == 0:
                            pe.wait_ge(m["sp_ready"], 2 * i + j // HB + 1)
                        w, at = slice(j * P, (j + 1) * P), e % 2
                        pe.matmul(ps_o[:, :], w2lo[:, e, w], sphi[:, at, j, :], start=(j == 0), stop=False)
                        pe.matmul(ps_o[:, :], w2hi[:, e, w], splo[:, at, j, :], start=False, stop=False)
                        mm = pe.matmul(ps_o[:, :], w2hi[:, e, w], sphi[:, at, j, :], start=False, stop=(j == HC - 1))
                    mm.then_inc(m["o_ready"], 1)

                turn_keys(0)
                turn_input(0)
                pe.wait_ge(s["cols_ready"], 1)
                pe.wait_ge(s["kT_ready"], 1)
                for tile in range(TG):
                    if tile == 2:
                        pe.wait_ge(s["ga_copied"], 1)
                    scores(0, tile)
                turn_probs(0, 0)
                turn_keys(1)
                turn_probs(0, 1)
                pe.wait_ge(s["kfac_ready"], B)
                pe.wait_ge(s["vg_ready"], 1)
                sums(0, range(0, 1))
                turn_keys(2)
                turn_probs(0, 2)
                sums(0, range(1, 2))
                turn_keys(3)
                turn_probs(0, 3)
                sums(0, range(2, 3))
                sums(0, range(3, 4))
                turn_input(1)
                pe.wait_ge(s["x2_done"], 1)
                for tile in range(TG):
                    scores(1, tile)
                turn_probs(1, 0)
                turn_input2(0)
                turn_probs(1, 1)
                pe.wait_ge(router_in, 32)
                logits(0)
                turn_probs(1, 2)
                turn_probs(1, 3)
                up(0, 0)
                pe.wait_ge(s["kT_ready"], B)
                pe.wait_ge(s["vg_ready"], B)

                def round_(g, before, att, inp, soft=True):
                    soft = soft and att
                    n = g + 1
                    for e in range(E):
                        if e == 0:
                            turn_gates(g, att)
                        if soft:
                            if e == 0:
                                scores(n, 0)
                                scores(n, 1)
                            if e == 1:
                                turn_probs(n, 0)
                                scores(n, 2)
                            if e == 2:
                                turn_probs(n, 2)
                        if att:
                            if e == 3:
                                sums(n)
                            if e == 6:
                                logits(n)
                        if before and e == 7 and not att:
                            turn_out(g - 1, s["gT_ready"], NG)
                        if e < E - 1:
                            up(g, e + 1)
                        elif att:
                            up(n, 0)
                        if soft:
                            if e == 1:
                                turn_probs(n, 1)
                                scores(n, 3)
                            if e == 2:
                                turn_probs(n, 3)
                        if att:
                            if e == 5:
                                turn_input2(n)
                            if e == 6 and before:
                                turn_out(g - 1, s["lg_ready"], n + 1)
                            if e == 7 and inp:
                                turn_input(n + 1)
                        down(g, e)

                rounds(pe, round_)
                turn_out(NG - 1, m["y_done"], NG - 1)

            @block.scalar
            def _(act):
                act.dma_start(xk[:, :], xk_dram).then_inc(xk_in, 16)
                act.dma_start(wm_sb[:, WM_A:], wmod[:, WM_A:]).then_inc(wm_in[1], 16)
                def table(func, at):
                    act.activation(warm[:, at:at + 1], mhalf[:, 0:1], func)

                act.wait_ge(s["zeroed"], 1)
                table(ACT.Exp, 0)
                act.wait_ge(s["cc_ready"], 1)
                act.activation(sil[:, 0, :], cc[:, :], ACT.Exp, scale=-1.0).then_inc(s["cexp"], 1)
                act.dma_start(k_sb[:, :, :], k_dram).then_inc(k_in, 16)
                act.dma_start(v_sb[:, :].rearrange("p (n d) -> p n d", d=D), v_dram).then_inc(v_in, 16)
                act.dma_start(wr_sb[:, :], Wr).then_inc(router_in, 16)
                act.dma_start(br_sb[:, :], br.rearrange("(a e) -> a e", a=1).broadcast_to([P, E])).then_inc(router_in, 16)

                def input_T(n):
                    if first(n):
                        act.wait_ge(s["mod_ready"], 1)
                        act.wait_ge(s["ht_ps"], 1)
                        cols_of = [mod[:, mo, 0:1] for mo in (SA, CA)]
                    else:
                        wait_all(act, s["modg_ready"], 1, (s["ht_ps"], n + 1), (s["scores_ready"], TG * n))
                        cols_of = [col_of(mo, n) for mo in (SA, CA)]
                    act.activation(ht[:, :], ps_x[:, :], ACT.Identity, bias=cols_of[0], scale=cols_of[1]).then_inc(s["ht_ready"], 1)

                def exps(n, t):
                    if t == 0 and not first(n):
                        act.wait_ge(s["rinv_ready"], n)
                    act.wait_ge(s["nmax_ready"], TG * n + t + 1)
                    act.activation(probs[:, t % 2, :], scores_bank(n, t)[:, :], ACT.Exp, bias=nmax[:, t:t + 1],
                                   accum_out=rsum[:, t:t + 1]).then_inc(s["exp_done"], 1)

                def probs_T(n, t):
                    act.wait_ge(s["pt_ps"], TG * n + t + 1)
                    act.activation(pt[:, :, t * P:(t + 1) * P], turned_bank(n, t)[:, :].rearrange("p (c n) -> p c n", c=KC),
                                   ACT.Copy).then_inc(s["pt_ready"], 1)

                def input2_T(n):
                    wait_all(act, s["modg_ready"], 1, (s["h2_ps"], n + 1), *([] if first(n) else [(s["h2_split"], n)]))
                    act.activation(h2[:, :], ps_x[:, :], ACT.Identity, bias=col_of(SB, n),
                                   scale=col_of(CB, n)).then_inc(s["h2_ready"], 1)

                def gate_exp(n):
                    act.wait_ge(s["dlt_ready"], n + 1)
                    if not first(n):
                        act.wait_ge(s["em_ready"], n)
                    act.activation(ex[:, :, :], dlt[:, :, :], ACT.Exp).then_inc(s["ex_ready"], 1)

                def gates_T(n):
                    act.wait_ge(s["gT_ps"], n + 1)
                    if not first(n):
                        for i in range(GS):
                            act.wait_ge(gbc_in[i], 16 * (E // GS) * n)
                    act.activation(gT[:, :], ps_x[0:E, :], ACT.Copy).then_inc(s["gT_ready"], 1)

                def hi_w(i):
                    act.wait_ge(w_in[i], 16 if i % 2 == 0 else 16 * EW)
                    act.activation(piece(w1hi, w2hi, i), raw[i],
                                   ACT.Copy).then_inc(s["w_hi"], 1)

                def keys_T(b):
                    act.wait_ge(s["ks_ps"], b + 1)
                    act.activation(kT[:, b * T:(b + 1) * T], ps_k[b][:, :], ACT.Copy).then_inc(s["kT_ready"], 1)

                def gelus(g, e):
                    i = E * g + e
                    for j in range(HC):
                        act.wait_ge(m["u_ready"], HC * i + j + 1)
                        if j % HB == 0 and not (first(g) and e < 2):
                            act.wait_ge(m["sp_ready"], 2 * (i - 2) + j // HB + 1)
                        n = e * HC + j
                        act.activation(gel[:, e % 2, j, :], ps_u[j][:, :], ACT.Gelu,
                                       bias=b1c[:, n:n + 1]).then_inc(m["gel_ready"], 1)

                keys_T(0)
                input_T(0)
                act.wait_ge(s["ga_ps"], 1)
                act.activation(ga_raw[:, :], ps_ga[:, :], ACT.Copy).then_inc(s["ga_copied"], 1)
                exps(0, 0)
                exps(0, 1)
                probs_T(0, 0)
                exps(0, 2)
                keys_T(1)
                probs_T(0, 1)
                exps(0, 3)
                keys_T(2)
                probs_T(0, 2)
                hi_w(0)
                probs_T(0, 3)
                keys_T(3)
                hi_w(1)
                input_T(1)
                hi_w(2)
                hi_w(3)
                exps(1, 0)
                exps(1, 1)
                probs_T(1, 0)
                input2_T(0)
                exps(1, 2)
                probs_T(1, 1)
                exps(1, 3)
                probs_T(1, 2)
                gate_exp(0)
                probs_T(1, 3)
                table(ACT.Gelu, 1)
                gelus(0, 0)
                hi_w(4)

                def round_(g, before, att, inp, soft=True):
                    soft = soft and att
                    n = g + 1
                    for e in range(E):
                        if e == 0:
                            gates_T(g)
                        if soft:
                            if e == 1:
                                probs_T(n, 0)
                            if e == 2:
                                probs_T(n, 2)
                        if e < E - 1:
                            gelus(g, e + 1)
                        elif att:
                            gelus(n, 0)
                        if soft:
                            if e == 0:
                                table(ACT.Exp, 0)
                                exps(n, 0)
                                exps(n, 1)
                                table(ACT.Gelu, 1)
                            if e == 1:
                                probs_T(n, 1)
                                table(ACT.Exp, 0)
                                exps(n, 2)
                                exps(n, 3)
                                table(ACT.Gelu, 1)
                            if e == 2:
                                probs_T(n, 3)
                        if att and e == 5:
                            input2_T(n)
                        if inp and e == 7:
                            input_T(n + 1)
                        if att and e == 6:
                            table(ACT.Exp, 0)
                            gate_exp(n)
                            table(ACT.Gelu, 1)
                        if first(g) and e < 3:
                            hi_w(5 + e)

                rounds(act, round_)

            @block.vector
            def _(dve):
                dve.wait_ge(s["c_T"], 1)
                dve.tensor_copy(cc[:, :], ps_c[:, 0:B]).then_inc(s["cc_ready"], 1)
                dve.wait_ge(xk_in, 16)
                dve.bn_stats(kst[:, :], xk[:, :]).then_inc(s["k_stat"], 1)
                dve.wait_ge(s["k_stat"], 1)
                dve.bn_aggr(kmv[:, 0:2], kst[:, :]).then_inc(s["k_aggr"], 1)
                dve.wait_ge(s["k_aggr"], 1)
                dve.tensor_scalar(kmv[:, 2:3], kmv[:, 1:2], EPS, None, ALU.add).then_inc(s["k_var"], 1)
                dve.wait_ge(s["cexp"], 1)
                dve.tensor_scalar(sil[:, 1, :], sil[:, 0, :], 1.0, None, ALU.add).then_inc(s["c1"], 1)
                dve.wait_ge(s["c1"], 1)
                dve.reciprocal(sil[:, 0, :], sil[:, 1, :]).then_inc(s["crec"], 1)
                dve.wait_ge(s["crec"], 1)
                dve.wait_ge(s["cc_ready"], 1)
                dve.tensor_tensor(sil[:, 2, :], cc[:, :], sil[:, 0, :], ALU.mult).then_inc(s["sil_ready"], 1)
                dve.wait_ge(s["k_rstd"], 1)
                dve.tensor_scalar(xkh[:, :], xk[:, :], kmv[:, 0:1], kmv[:, 3:4], ALU.subtract, ALU.mult).then_inc(s["xkh_ready"], 1)

                def modulation():
                    dve.wait_ge(s["mod_ps"], 1)
                    dve.tensor_copy(mod[:, SA, :], ps_mod[:, 0:B])
                    dve.tensor_scalar(mod[:, CA, :], ps_mod[:, B:2 * B], 1.0, None, ALU.add).then_inc(s["mod_ready"], 1)

                def modulation_of_groups():
                    dve.wait_ge(s["mod_ps"], 2)
                    dve.tensor_copy(mod[:, SB:GBM + 1, :],
                                    ps_mod2[:, SB * B:(GBM + 1) * B].rearrange("p (m b) -> p m b", b=B)).then_inc(s["mod_copied"], 1)
                    dve.wait_ge(s["mod_copied"], 1)
                    dve.tensor_scalar(mod[:, CB, :], mod[:, CB, :], 1.0, None, ALU.add).then_inc(s["mod_step"], 1)
                    dve.tensor_scalar(gsgn[:, 0, :], mod[:, GBM, :], 0.0, 2.0, ALU.is_ge, ALU.mult).then_inc(s["mod_step"], 1)
                    dve.scalar_tensor_tensor(out=gsgn[:, 1, :], in0=mod[:, GBM, :], scalar=-1.0, in1=mod[:, GBM, :],
                                             op0=ALU.mult, op1=ALU.max).then_inc(s["mod_step"], 1)
                    dve.wait_ge(s["mod_step"], 3)
                    dve.tensor_scalar(gsgn[:, 0, :], gsgn[:, 0, :], -1.0, None, ALU.add).then_inc(s["mod_step"], 1)
                    dve.tensor_scalar(gsgn[:, 1, :], gsgn[:, 1, :], 0.25, None, ALU.max).then_inc(s["mod_step"], 1)
                    dve.wait_ge(s["mod_step"], 5)
                    dve.tensor_tensor(mod[:, GBM, :], gsgn[:, 0, :], gsgn[:, 1, :], ALU.mult).then_inc(s["mod_ready"], 1)
                    dve.wait_ge(s["mod_ready"], 2)
                    for g in range(GB):
                        op = dve.tensor_copy(mod_g[:, :, :].rearrange("p m (b g) -> p m b g", g=GB)[:, :, :, g], mod[:, :, :])
                    op.then_inc(s["modg_ready"], 1)

                def key_factors(b):
                    dve.wait_ge(s["kfac_ps"], 1)
                    dve.wait_ge(s["mod_ready"], 1)
                    dve.tensor_scalar(kfac[:, b, :], ps_kfac[:, b * KC:(b + 1) * KC], mod[:, CA, b:b + 1],
                                      mod[:, SA, b:b + 1], ALU.mult, ALU.add).then_inc(s["kfac_ready"], 1)

                def scale_keys(b):
                    dve.wait_ge(k_in, 16)
                    key_factors(b)
                    dve.wait_ge(s["kfac_ready"], b + 1)
                    for j in range(KC):
                        op = dve.tensor_scalar(ks[:, b, j, :], k_sb[:, j, :], kfac[:, b, j:j + 1], None, ALU.mult)
                    op.then_inc(s["ks_ready"], 1)

                def ga_rows():
                    dve.wait_ge(s["ga_copied"], 1)
                    dve.tensor_scalar(ga_sign, ga_raw[:, :], 0.0, 2.0, ALU.is_ge, ALU.mult).then_inc(s["ga_step"], 1)
                    dve.scalar_tensor_tensor(out=ga_abs, in0=ga_raw[:, :], scalar=-1.0, in1=ga_raw[:, :],
                                             op0=ALU.mult, op1=ALU.max).then_inc(s["ga_step"], 1)
                    dve.wait_ge(s["ga_step"], 2)
                    dve.tensor_scalar(ga_abs, ga_abs, 0.25, None, ALU.max).then_inc(s["ga_step"], 1)
                    dve.wait_ge(s["ga_step"], 3)
                    dve.scalar_tensor_tensor(out=ga_raw[:, :], in0=ga_sign, scalar=-1.0, in1=ga_abs,
                                             op0=ALU.add, op1=ALU.mult).then_inc(s["ga_step"], 1)

                def tile_of(n, t):
                    if isinstance(n, int):
                        return x_sb[:, TG * n + t, :]
                    return x_sb[:, bass.ds(TG * n + t, 1), :].rearrange("p a d -> p (a d)")

                def stats(which, n):
                    i = which - 1
                    before = [] if first(n) else [(s[f"aggr{which}"], TG * n)]
                    if which == 2:
                        before.append((s["x2_done"], n + 1))
                    wait_all(dve, x_in[0], 16, *before)
                    for t in range(TG):
                        dve.bn_stats(st[:, i, t, :], tile_of(n, t)).then_inc(s[f"stat{which}"], 1)
                    wait_all(dve, x_in[0], 16, (s[f"stat{which}"], TG * n + TG),
                             *([] if first(n) else [(s[f"xhat{which}"], n)]))
                    for t in range(TG):
                        dve.bn_aggr(mv[:, i, t, :], st[:, i, t, :]).then_inc(s[f"aggr{which}"], 1)
                    dve.wait_ge(s[f"aggr{which}"], TG * n + TG)
                    dve.tensor_scalar(veps[:, i, :], mv[:, i, :, 1], EPS, None, ALU.add).then_inc(s[f"var{which}"], 1)

                def normalize(which, n):
                    i = which - 1
                    dve.wait_ge(s[f"rstd{which}"], n + 1)
                    if not first(n):
                        dve.wait_ge(s[("ht_ps", "h2_ps")[i]], n)
                    for t in range(TG):
                        op = dve.tensor_scalar(xh[:, i, t, :], tile_of(n, t), mv[:, i, t, 0:1], rstd[:, i, t:t + 1],
                                               ALU.subtract, ALU.mult)
                    op.then_inc(s[f"xhat{which}"], 1)

                def maxima(n, t):
                    dve.wait_ge(s["scores_ready"], TG * n + t + 1)
                    dve.tensor_reduce(nmax[:, t:t + 1], scores_bank(n, t)[:, :], AX_X, ALU.max,
                                      negate=True).then_inc(s["nmax_ready"], 1)

                def denominators(n):
                    dve.wait_ge(s["exp_done"], TG * (n + 1))
                    if not first(n):
                        dve.wait_ge(s["x2_done"], n)
                    dve.reciprocal(rinv[:, :], rsum[:, :]).then_inc(s["rinv_ready"], 1)

                def residual(n):
                    dve.wait_ge(s["pv_done"], TG * (n + 1))
                    dve.wait_ge(s["rinv_ready"], n + 1)
                    for t in range(TG):
                        xt = tile_of(n, t)
                        op = dve.scalar_tensor_tensor(out=xt, in0=sums_bank(n, t)[:, t * P:(t + 1) * P], scalar=rinv[:, t:t + 1],
                                                      in1=xt, op0=ALU.mult, op1=ALU.add)
                    op.then_inc(s["x2_done"], 1)

                def residual_and_stats(n):
                    dve.wait_ge(s["rinv_ready"], n + 1)
                    for t in range(TG):
                        dve.wait_ge(s["pv_done"], t + 1)
                        xt = tile_of(n, t)
                        dve.scalar_tensor_tensor(out=xt, in0=sums_bank(n, t)[:, t * P:(t + 1) * P], scalar=rinv[:, t:t + 1],
                                                 in1=xt, op0=ALU.mult, op1=ALU.add).then_inc(
                                                     s["x2_done" if t == TG - 1 else "x2_tile"], 1)
                        dve.wait_ge(*(s["x2_done"], 1) if t == TG - 1 else (s["x2_tile"], t + 1))
                        dve.bn_stats(st[:, 1, t, :], xt).then_inc(s["stat2"], 1)
                        dve.wait_ge(s["stat2"], t + 1)
                        dve.bn_aggr(mv[:, 1, t, :], st[:, 1, t, :]).then_inc(s["aggr2"], 1)
                    dve.wait_ge(s["aggr2"], TG)
                    dve.tensor_scalar(veps[:, 1, :], mv[:, 1, :, 1], EPS, None, ALU.add).then_inc(s["var2"], 1)

                def hi_input(n):
                    dve.wait_ge(s["h2_ready"], n + 1)
                    dve.tensor_copy(slot_cols(h2hi, n), h2[:, :]).then_inc(s["h2_hi"], 1)

                def gate_logits(n):
                    dve.wait_ge(s["log_ps"], n + 1)
                    dve.wait_ge(router_in, 32)
                    dve.tensor_tensor(lg[:, :, :], ps_x[:, 0:TG * E].rearrange("p (t e) -> p t e", e=E),
                                      br_sb[:, :].unsqueeze(1).to_broadcast([P, TG, E]), ALU.add).then_inc(s["lg_ready"], 1)
                    wait_all(dve, router_in, 32, (s["lg_ready"], n + 1))
                    for t in range(TG):
                        op = dve.max(top[:, t, :], lg[:, t, :])
                    op.then_inc(s["top_ready"], 1)
                    dve.wait_ge(s["top_ready"], n + 1)
                    dve.tensor_tensor(dlt[:, :, :], lg[:, :, :], top[:, :, 0:1].to_broadcast([P, TG, E]),
                                      ALU.subtract).then_inc(s["dlt_ready"], 1)
                    dve.tensor_tensor(keep[:, :, :], lg[:, :, :], top[:, :, 1:2].to_broadcast([P, TG, E]),
                                      ALU.is_ge).then_inc(s["keep_ready"], 1)

                def gate_weights(n):
                    dve.wait_ge(s["ex_ready"], n + 1)
                    dve.wait_ge(s["keep_ready"], n + 1)
                    dve.tensor_tensor(em[:, :, :], ex[:, :, :], keep[:, :, :], ALU.mult).then_inc(s["em_ready"], 1)
                    dve.wait_ge(s["em_ready"], n + 1)
                    dve.tensor_reduce(esum[:, :], em[:, :, :], AX_X, ALU.add).then_inc(s["esum_ready"], 1)
                    dve.wait_ge(s["esum_ready"], n + 1)
                    dve.reciprocal(einv[:, :], esum[:, :]).then_inc(s["einv_ready"], 1)
                    dve.wait_ge(s["einv_ready"], n + 1)
                    if not first(n):
                        dve.wait_ge(s["gT_ps"], n)
                    dve.tensor_tensor(wgt[:, :, :], em[:, :, :], einv[:, :].unsqueeze(2).to_broadcast([P, TG, E]),
                                      ALU.mult).then_inc(s["wgt_ready"], 1)

                def split(g, e, half):
                    i = E * g + e
                    c = slice(half * HB, (half + 1) * HB)
                    dve.wait_ge(m["gel_ready"], HC * i + (half + 1) * HB)
                    dve.tensor_copy(sphi[:, e % 2, c, :], gel[:, e % 2, c, :]).then_inc(m["sp_hi"], 1)
                    dve.wait_ge(m["sp_hi"], 2 * i + half + 1)
                    dve.tensor_tensor(splo[:, e % 2, c, :], gel[:, e % 2, c, :], sphi[:, e % 2, c, :].bitcast(F32),
                                      ALU.subtract).then_inc(m["sp_ready"], 1)

                def gate(g, e):
                    i = E * g + e
                    dve.wait_ge(m["o_ready"], i + 1)
                    dve.wait_ge(gbc_in[e % GS], 16 * ((E // GS) * g + e // GS + 1))
                    if e == 0:
                        if not first(g):
                            dve.wait_ge(m["outT_done"], g)
                    elif not (first(g) and e <= 2):
                        dve.wait_ge(m["added"], (E - 1) * g + max(e - 2, 0))
                    dve.scalar_tensor_tensor(out=acc[:, :] if e == 0 else msk[:, e % 2, :], in0=ps_o[:, :],
                                             scalar=b2c[:, e:e + 1], in1=gbc[:, e % GS, :],
                                             op0=ALU.add, op1=ALU.mult).then_inc(m["gated"], 1)

                def finish(g):
                    dve.wait_ge(m["fin_ps"], ONE + g + 1)
                    at = group_tiles(g)
                    dve.tensor_tensor(x_sb[:, at, :], ps_x[:, :].rearrange("p (t d) -> p t d", d=D), x_sb[:, at, :],
                                      ALU.add).then_inc(m["y_done"], 1)

                def split_w2(i):
                    dve.wait_ge(s["w_hi"], 2 * i + 2)
                    dve.tensor_tensor(piece(w1lo, w2lo, 2 * i + 1), raw[2 * i + 1], piece(w1hi, w2hi, 2 * i + 1).bitcast(F32),
                                      ALU.subtract).then_inc(s["w2_split"], 1)

                modulation()
                dve.wait_ge(x_in[0], 16)
                stats(1, 0)
                scale_keys(0)
                normalize(1, 0)
                dve.wait_ge(s["rows_T"], 1)
                dve.tensor_copy(cols[:, :], ps_rows[:, 0:R]).then_inc(s["cols_ready"], 1)
                modulation_of_groups()
                scale_keys(1)
                ga_rows()
                maxima(0, 0)
                maxima(0, 1)
                scale_keys(2)
                maxima(0, 2)
                maxima(0, 3)
                scale_keys(3)
                dve.wait_ge(x1_in, 16)
                stats(1, 1)
                denominators(0)
                normalize(1, 1)
                residual_and_stats(0)
                maxima(1, 0)
                maxima(1, 1)
                normalize(2, 0)
                maxima(1, 2)
                hi_input(0)
                maxima(1, 3)
                split_w2(0)
                gate_logits(0)
                gate_weights(0)
                denominators(1)
                split_w2(1)
                split(0, 0, 0)
                split(0, 0, 1)
                for i in range(1, B):
                    dve.wait_ge(x_in[i], 16)

                def round_(g, before, att, inp, soft=True):
                    soft = soft and att
                    n = g + 1
                    for e in range(E):
                        ge, nexte = (g, e + 1) if e < E - 1 else (n, 0)
                        if soft:
                            if e == 0:
                                maxima(n, 0)
                                maxima(n, 1)
                            if e == 1:
                                maxima(n, 2)
                            if e == 2:
                                denominators(n)
                        if att:
                            if e == 2 and inp:
                                stats(1, n + 1)
                            if e == 3:
                                if inp:
                                    normalize(1, n + 1)
                                residual(n)
                                stats(2, n)
                        if att and e == 6:
                            gate_logits(n)
                        if e < E - 1 or att:
                            split(ge, nexte, 0)
                        if soft and e == 1:
                            maxima(n, 3)
                        if att:
                            if e == 4:
                                normalize(2, n)
                            if e == 5:
                                hi_input(n)
                            if e == 7:
                                gate_weights(n)
                        if e < E - 1 or att:
                            split(ge, nexte, 1)
                        if first(g) and e == 0:
                            dve.wait_ge(s["w1_split"], 3)
                        if before and e == (6 if att else 7):
                            finish(g - 1)
                        gate(g, e)
                        if first(g) and e in (0, 2):
                            split_w2(2 + e // 2)

                rounds(dve, round_)
                dve.wait_ge(m["gated"], E * NG)
                dve.wait_ge(m["added"], (E - 1) * NG - 1)
                dve.tensor_tensor(acc[:, :], acc[:, :], msk[:, (E - 1) % 2, :], ALU.add).then_inc(m["added"], 1)
                dve.wait_ge(m["added"], (E - 1) * NG)
                dve.wait_ge(m["fin_ps"], ONE + NG - 1)
                dve.tensor_scalar(outT[:, :], acc[:, :], col_of(GBM, NG - 1), None, ALU.mult).then_inc(m["outT_done"], 1)
                finish(NG - 1)


_INS = ['L0_attn_q', 'L0_attn_k', 'L0_attn_v', 'L0_ffn_W1', 'L0_ffn_b1', 'L0_ffn_W2', 'L0_ffn_b2',
        'L0_ffn_Wr', 'L0_ffn_br', 'L0_c', 'L0_wmod']


def kernel(**inputs):
    import numpy as _np
    import concourse.bacc as _bacc
    from concourse import mybir as _mybir
    from concourse.bass_utils import run_bass_kernel_spmd as _run

    nc = _bacc.Bacc("TRN2", target_bir_lowering=False, num_devices=1)
    arrays, args = {}, []
    for name in _INS:
        a = _np.ascontiguousarray(inputs[name])
        arrays[f"in_{name}_dram"] = a
        args.append(nc.dram_tensor(f"in_{name}_dram", a.shape, _mybir.dt.from_np(a.dtype), kind="ExternalInput").ap())
    out = nc.dram_tensor("out_0_dram", inputs['L0_attn_q'].shape, _mybir.dt.float32, kind="ExternalOutput").ap()
    adaln_block(nc, *args, out)
    r = _run(nc, [arrays], core_ids=[0])
    return r.results[0]["out_0_dram"]
```
